# Optimizing a Trainium2 kernel written in Bass

```python
import numpy as np
import jax
import jax.numpy as jnp

def _softmax(x, axis=-1):
    return jax.nn.softmax(x, axis=axis)

def _gelu(x):
    return jax.nn.gelu(x, approximate=True)

def _silu(x):
    return jax.nn.silu(x)

def _sigmoid(x):
    return jax.nn.sigmoid(x)

def _layernorm(x, axis=-1, eps=1e-05):
    m = jnp.mean(x, axis=axis, keepdims=True)
    v = jnp.var(x, axis=axis, keepdims=True)
    return (x - m) / jnp.sqrt(v + eps)

def _scatter_add(tgt, idx, src, axis=0):
    return tgt.at[idx].add(src)

def _segment_sum(src, seg, n):
    return jax.ops.segment_sum(src, seg, n)
kernel_name = 'mk_xattn_ffn_d1_seqx_r4_d8befa'

def setup_inputs(seed: int=0):
    np.random.seed(seed)
    _w = jnp.asarray

    def _rec_inputs():
        import jax
        import jax.numpy as jnp
        _rk = jax.random.key(seed)
        x = 0.000341 + 1 * jax.random.normal(jax.random.fold_in(_rk, 1), (8, 256, 512), jnp.float32)
        _lenS = 256 - jax.random.randint(jax.random.fold_in(_rk, 7), (8,), 0, max(1, 256 // 4) + 1, jnp.int32)
        _lenS2 = 256 - jax.random.randint(jax.random.fold_in(_rk, 8), (8,), 0, max(1, 256 // 4) + 1, jnp.int32)
        _ctx_2048P = jax.random.normal(jax.random.fold_in(_rk, 11), (8, 16, 512), jnp.float32)
        _ctx_2048c = jax.random.dirichlet(jax.random.fold_in(_rk, 511), 0.3 * jnp.ones((16,), jnp.float32), (8, 256))
        _ctx_2048t = jnp.einsum('bsk,bkd->bsd', _ctx_2048c, _ctx_2048P)
        _ctx_2048t = _ctx_2048t * jax.lax.rsqrt(jnp.mean(jnp.square(_ctx_2048t)) + 1e-12) * 0.953939
        ctx_2048 = -1.47943e-05 + 1.00017 * (_ctx_2048t + 0.3 * jax.random.normal(jax.random.fold_in(_rk, 611), (8, 256, 512), jnp.float32))
        return (x, ctx_2048)
    x, ctx_2048 = _rec_inputs()

    def _L0_xattn_setup():
        import jax, jax.numpy as jnp
        import numpy as np

        def _wkv(time_decay, time_first, k, v):
            w = -jnp.exp(time_decay)
            u = time_first
            B, T, C = k.shape
            aa = jnp.zeros((B, C), dtype=k.dtype)
            bb = jnp.zeros((B, C), dtype=k.dtype)
            pp = jnp.full((B, C), -1e+38, dtype=k.dtype)

            def step(carry, kv_t):
                aa, bb, pp = carry
                kt, vt = kv_t
                ww = u + kt
                q = jnp.maximum(pp, ww)
                e1 = jnp.exp(pp - q)
                e2 = jnp.exp(ww - q)
                y_t = (e1 * aa + e2 * vt) / (e1 * bb + e2)
                ww2 = pp + w
                q2 = jnp.maximum(ww2, kt)
                e1b = jnp.exp(ww2 - q2)
                e2b = jnp.exp(kt - q2)
                new_carry = (e1b * aa + e2b * vt, e1b * bb + e2b, q2)
                return (new_carry, y_t)
            ks = jnp.transpose(k, (1, 0, 2))
            vs = jnp.transpose(v, (1, 0, 2))
            _, ys = jax.lax.scan(step, (aa, bb, pp), (ks, vs))
            return jnp.transpose(ys, (1, 0, 2))
        key = jax.random.key(seed)
        k1, k2, k3, k4 = jax.random.split(key, 4)
        B, T, C = (8, 256, 512)
        return {'batch_size': B, 'seq_len': T, 'embedding_dim': C, 'time_decay': jax.random.normal(k1, (C,), dtype=jnp.float32), 'time_first': jax.random.normal(k2, (C,), dtype=jnp.float32), 'k': jax.random.normal(k3, (B, T, C), dtype=jnp.float32), 'v': jax.random.normal(k4, (B, T, C), dtype=jnp.float32)}
    _L0_xattn_all = _L0_xattn_setup()
    _L0_xattn_in = {k: v for k, v in _L0_xattn_all.items() if k in ('time_decay', 'time_first')}
    del _L0_xattn_all

    def _L0_ffn_setup():
        import jax, jax.numpy as jnp
        import numpy as np
        B, S, D = (2, 1024, 512)
        E, DFF = (8, 2048)
        TOP_K = 2
        key = jax.random.key(seed)
        ks = jax.random.split(key, 4)
        scale_in = 1.0 / np.sqrt(D)
        scale_ff = 1.0 / np.sqrt(DFF)
        return {'hidden_states': jax.random.normal(ks[0], (B, S, D), dtype=jnp.float32), 'gate_w': jax.random.normal(ks[1], (E, D), dtype=jnp.float32) * scale_in, 'w1': jax.random.normal(ks[2], (E, D, DFF), dtype=jnp.float32) * scale_in, 'b1': jnp.zeros((E, DFF), dtype=jnp.float32), 'w2': jax.random.normal(ks[3], (E, DFF, D), dtype=jnp.float32) * scale_ff, 'b2': jnp.zeros((E, D), dtype=jnp.float32)}
    _L0_ffn_all = _L0_ffn_setup()
    _L0_ffn_in = {k: v for k, v in _L0_ffn_all.items() if k in ('gate_w', 'w1', 'b1', 'w2', 'b2')}
    del _L0_ffn_all
    return {'x': x, 'ctx_2048': ctx_2048, 'L0_xattn_time_decay': _L0_xattn_in['time_decay'], 'L0_xattn_time_first': _L0_xattn_in['time_first'], 'L0_ffn_gate_w': _L0_ffn_in['gate_w'], 'L0_ffn_w1': _L0_ffn_in['w1'], 'L0_ffn_b1': _L0_ffn_in['b1'], 'L0_ffn_w2': _L0_ffn_in['w2'], 'L0_ffn_b2': _L0_ffn_in['b2']}

def reference(x, ctx_2048, L0_xattn_time_decay, L0_xattn_time_first, L0_ffn_gate_w, L0_ffn_w1, L0_ffn_b1, L0_ffn_w2, L0_ffn_b2):
    import jax
    import jax.numpy as jnp

    def _L0_xattn_ref(batch_size, seq_len, embedding_dim, time_decay, time_first, k, v):
        import jax, jax.numpy as jnp
        import numpy as np

        def _wkv(time_decay, time_first, k, v):
            w = -jnp.exp(time_decay)
            u = time_first
            B, T, C = k.shape
            aa = jnp.zeros((B, C), dtype=k.dtype)
            bb = jnp.zeros((B, C), dtype=k.dtype)
            pp = jnp.full((B, C), -1e+38, dtype=k.dtype)

            def step(carry, kv_t):
                aa, bb, pp = carry
                kt, vt = kv_t
                ww = u + kt
                q = jnp.maximum(pp, ww)
                e1 = jnp.exp(pp - q)
                e2 = jnp.exp(ww - q)
                y_t = (e1 * aa + e2 * vt) / (e1 * bb + e2)
                ww2 = pp + w
                q2 = jnp.maximum(ww2, kt)
                e1b = jnp.exp(ww2 - q2)
                e2b = jnp.exp(kt - q2)
                new_carry = (e1b * aa + e2b * vt, e1b * bb + e2b, q2)
                return (new_carry, y_t)
            ks = jnp.transpose(k, (1, 0, 2))
            vs = jnp.transpose(v, (1, 0, 2))
            _, ys = jax.lax.scan(step, (aa, bb, pp), (ks, vs))
            return jnp.transpose(ys, (1, 0, 2))
        assert seq_len <= 256
        return _wkv(time_decay, time_first, k, v)

    def _L0_ffn_ref(hidden_states, gate_w, w1, b1, w2, b2):
        import jax, jax.numpy as jnp
        import numpy as np
        B, S, D = (2, 1024, 512)
        E, DFF = (8, 2048)
        TOP_K = 2
        b, s, d = hidden_states.shape
        x = hidden_states.reshape(-1, d)
        router_logits = x @ gate_w.T
        _, sel = jax.lax.top_k(router_logits.sum(axis=0), TOP_K)
        rw = jax.nn.softmax(router_logits[:, sel].astype(jnp.float32), axis=1)
        rw = rw.astype(x.dtype)
        w1s, b1s = (w1[sel], b1[sel])
        w2s, b2s = (w2[sel], b2[sel])
        h = jax.nn.gelu(jnp.einsum('nd,kdf->knf', x, w1s) + b1s[:, None, :])
        y = jnp.einsum('knf,kfd->knd', h, w2s) + b2s[:, None, :]
        out = jnp.einsum('nk,knd->nd', rw, y)
        return out.reshape(b, s, -1)
    x = x + _L0_xattn_ref(8, 256, 512, L0_xattn_time_decay, L0_xattn_time_first, _layernorm(x, axis=-1), ctx_2048)
    x = x + _L0_ffn_ref(_layernorm(x, axis=-1), L0_ffn_gate_w, L0_ffn_w1, L0_ffn_b1, L0_ffn_w2, L0_ffn_b2)
    return x

_drawn_inputs = setup_inputs


def setup_inputs(seed=0):
    import zlib

    import numpy as np

    out = dict(_drawn_inputs(seed))
    spreads = {'L0_ffn_b1': (0.0, 0.1), 'L0_ffn_b2': (0.0, 0.1)}
    factors = {}
    for name, (base, spread) in spreads.items():
        noise = np.random.default_rng([zlib.crc32(name.encode()), seed]).standard_normal(out[name].shape)
        drawn = base * np.exp(spread * noise) if base else spread * noise
        out[name] = jnp.asarray(drawn.astype(out[name].dtype))
    for name, factor in factors.items():
        out[name] = (out[name] * factor).astype(out[name].dtype)
    return out
```

```python
from contextlib import ExitStack

import concourse.bass as bass
from concourse import mybir

P = 128
F32 = mybir.dt.float32
F16 = mybir.dt.float16
BF16 = mybir.dt.bfloat16
I32 = mybir.dt.int32
U32 = mybir.dt.uint32
ALU = mybir.AluOpType
ACT = mybir.ActivationFunctionType
AX_X = mybir.AxisListType.X
AX_XY = mybir.AxisListType.XY

LN_EPS = 1e-5
X_SCALE = 1024.0


def wait(eng, sem, value):
    if not (isinstance(value, int) and value <= 0):
        eng.wait_ge(sem, value)


def wkv_moe_kernel(nc, x, ctx_in, time_decay, time_first, gate_w, w1, b1, w2, b2, out):
    B, T, C = x.shape
    E, _, DFF = w1.shape
    TOPK = 2
    N = B * T
    TILES = N // P
    CT = C // P
    GB = 4
    GT = GB * P
    NG = TILES // GB
    RB = GT // T
    SEG = T + 1
    FC = 512
    FT = FC // P
    CPE = DFF // FC
    NCH = TOPK * CPE
    NB = N // GT
    assert NB == 4 and FT == 4 and CT == 4 and GB == 4 and C == 512 and NCH % 2 == 0

    x_v = x.rearrange("b t c -> (b t) c").rearrange("(n p) c -> p n c", p=P)
    v_v = ctx_in.rearrange("b t c -> (b t) c").rearrange("(n p) c -> p n c", p=P)
    out_v = out.rearrange("b t c -> (b t) c").rearrange("(n p) c -> p n c", p=P)

    with ExitStack() as ctx:
        def sb(name, shape, dt):
            return ctx.enter_context(nc.sbuf_tensor(name, shape, dt))

        def sem(name):
            return ctx.enter_context(nc.semaphore(name))

        xa = sb("xa", [P, TILES, C], F32)
        xh = sb("xh", [P, CT, N], F16)
        xl = sb("xl", [P, CT, N], F16)
        stage1 = sb("stage1", [P, CT, FC], F32)
        stage2 = sb("stage2", [P, FT, C], F32)
        ident = sb("ident", [P, P], F32)
        ones = sb("ones", [P, P], F32)
        rows = sb("rows", [P, P], F32)
        b1rows = sb("b1rows", [P, P], F32)
        gate_rows = sb("gate_rows", [E, C], F32)
        cols = sb("cols", [P, 2 * CT], F32)
        edec = sb("edec", [P, CT], F32)
        dcol = sb("dcol", [P, CT], F32)
        um = sb("um", [P, CT], F32)
        nup = sb("nup", [P, CT], F32)
        mask = sb("mask", [P, RB * SEG], F32)
        decay = sb("decay", [P, CT, RB * SEG], F32)
        eps = sb("eps", [P, 1], F32)
        b1T = sb("b1T", [P, E, DFF // P], F32)
        gT = sb("gT", [P, CT, E], F32)
        gres = sb("gres", [P, 2, CT, E], F32)
        g3 = sb("g3", [P, CT, 3, E], BF16)
        bn = sb("bn", [P, GB, 6], F32)
        mv = sb("mv", [P, TILES, 2], F32)
        lnv = sb("lnv", [P, TILES], F32)
        rstd = sb("rstd", [P, TILES], F32)
        nmr = sb("nmr", [P, TILES], F32)
        sm = sb("sm", [P, TILES], F32)
        nm = sb("nm", [P, TILES], F32)
        ssq = sb("ssq", [P, TILES], F32)
        lnv2 = sb("lnv2", [P, TILES], F32)
        rs2 = sb("rs2", [P, TILES], F32)
        logits = sb("logits", [P, TILES, E], F32)
        tot = sb("tot", [P, E], F32)
        top = sb("top", [P, 8], F32)
        topi = sb("topi", [P, 8], U32)
        topf = sb("topf", [P, 8], F32)
        iota = sb("iota", [P, E], F32)
        pick = sb("pick", [P, TOPK, E], F32)
        lsel = sb("lsel", [P, TOPK, TILES], F32)
        lmax = sb("lmax", [P, TILES], F32)
        lexp = sb("lexp", [P, TOPK, TILES], F32)
        lsum = sb("lsum", [P, TILES], F32)
        linv = sb("linv", [P, TILES], F32)
        rw = sb("rw", [P, TOPK, TILES], F32)
        ptmp = sb("ptmp", [P, TILES, E], F32)
        b1tmp = sb("b1tmp", [P, DFF // P, E], F32)
        b1c = sb("b1c", [P, TOPK, DFF // P], F32)
        mb = sb("mb", [P, TOPK], F32)
        mb2 = sb("mb2", [P, NCH], F32)
        mx = sb("mx", [P, NCH, 2], F32)
        q = sb("q", [P, NCH, 3], F32)
        eb = sb("eb", [P, 2, 3], I32)
        eh = sb("eh", [P, 2, 3], I32)
        ei = sb("ei", [P, 2, 3], I32)
        scale = sb("scale", [P, 2, 3], F32)
        descale = sb("descale", [P, 2, 3], F32)
        gsc = sb("gsc", [P, 2], F32)
        bias = sb("bias", [P, 2, FT], F32)
        rwd = sb("rwd", [P, NCH, TILES], F32)

        TP = CT * RB * SEG
        TU = CT * GT
        arena_y = sb("arena_y", [P, NG * TU], F32)
        arena_v = sb("arena_v", [P, NG * TU], F32)
        arena_t = sb("arena_t", [P, 2 * TU + 2 * TP], F32)
        arena_s = sb("arena_s", [P, 3 * C], F32)
        kn = arena_y[:, :].rearrange("p (g t c) -> p g t c", g=NG, t=GB)
        yT = arena_y[:, :].rearrange("p (g k n) -> p g k n", g=NG, k=CT)
        vn = arena_v[:, :].rearrange("p (n c) -> p n c", c=C)
        ek = arena_t[:, 0:TU].rearrange("p (k n) -> p k n", k=CT)
        ekv = arena_t[:, TU:2 * TU].rearrange("p (k n) -> p k n", k=CT)
        s1 = arena_t[:, 2 * TU:2 * TU + TP].rearrange("p (k n) -> p k n", k=CT)
        sv = arena_t[:, 2 * TU + TP:2 * TU + 2 * TP].rearrange("p (k n) -> p k n", k=CT)
        x2n = arena_s[:, 0:2 * C].rearrange("p (a c) -> p a c", a=2)
        junk = arena_s[:, 2 * C:3 * C]
        yb = arena_y[:, :].bitcast(F16)
        WS = CT * FC
        w1h = yb[:, 0:2 * WS].rearrange("p (a k f) -> p a k f", a=2, k=CT)
        w1l = yb[:, 2 * WS:4 * WS].rearrange("p (a k f) -> p a k f", a=2, k=CT)
        w2h = yb[:, 4 * WS:6 * WS].rearrange("p (a k f) -> p a k f", a=2, k=FT)
        w2l = yb[:, 6 * WS:8 * WS].rearrange("p (a k f) -> p a k f", a=2, k=FT)
        vb = arena_v[:, :].bitcast(F16)
        HS = NB * FT * GT
        hh = vb[:, 0:HS].rearrange("p (n k t) -> p n k t", n=NB, k=FT)
        hl = vb[:, HS:2 * HS].rearrange("p (n k t) -> p n k t", n=NB, k=FT)
        g32 = arena_t[:, 0:FT * GT].rearrange("p (k t) -> p k t", k=FT)
        b2b = arena_t[:, TU:TU + TOPK * C].rearrange("p (k c) -> p k c", k=TOPK)
        bt = arena_t[:, TU + TOPK * C:TU + 2 * TOPK * C].rearrange("p (k c) -> p k c", k=TOPK)

        ps = ctx.enter_context(nc.psum_tensor("ps", [P, 8, 512], F32))
        psK = [ps[:, 0, :], ps[:, 1, :]]
        psV = [ps[:, 2, :], ps[:, 3, :]]
        psY = ps[:, 4, :]
        psX = [ps[:, 5, :], ps[:, 6, :]]
        psM = ps[:, 7, :]
        psA = [ps[:, n, :] for n in range(FT)]
        psB = [ps[:, 4, :], ps[:, 5, :]]
        psS = ps[:, 6, 0:3]

        d_x = [sem(f"d_x{g}") for g in range(NG)]
        d_v = [sem(f"d_v{g}") for g in range(NG)]
        d_rows = sem("d_rows")
        d_w1 = sem("d_w1")
        d_w2 = sem("d_w2")
        d_b2 = sem("d_b2")
        d_out = sem("d_out")
        x_landed = sem("x_landed")
        v_landed = sem("v_landed")
        c_pool = sem("c_pool")
        c_id = sem("c_id")
        c_cols = sem("c_cols")
        c_edec = sem("c_edec")
        c_dcol = sem("c_dcol")
        c_dve = sem("c_dve")
        c_gateT = sem("c_gateT")
        c_g3 = sem("c_g3")
        c_ready = sem("c_ready")
        bn_done = sem("bn_done")
        mv_ready = sem("mv_ready")
        lnv_done = sem("lnv_done")
        rstd_ready = sem("rstd_ready")
        nmr_ready = sem("nmr_ready")
        kn_ready = sem("kn_ready")
        kT_ready = sem("kT_ready")
        vT_ready = sem("vT_ready")
        ek_ready = sem("ek_ready")
        keys_ready = sem("keys_ready")
        sv_in = sem("sv_in")
        v_used = sem("v_used")
        sv_ready = sem("sv_ready")
        s1_ready = sem("s1_ready")
        num_done = sem("num_done")
        den_done = sem("den_done")
        lnd_done = sem("lnd_done")
        r_ready = sem("r_ready")
        y_done = sem("y_done")
        yT_ready = sem("yT_ready")
        x1_ready = sem("x1_ready")
        nm_ready = sem("nm_ready")
        sq_done = sem("sq_done")
        lnv2_done = sem("lnv2_done")
        rs2_ready = sem("rs2_ready")
        x2n_ready = sem("x2n_ready")
        x2T_ready = sem("x2T_ready")
        xh_ready = sem("xh_ready")
        xl_ready = sem("xl_ready")
        lg_mm = sem("lg_mm")
        lg_done = sem("lg_done")
        tot_mm = sem("tot_mm")
        rt = sem("rt")
        top_ready = sem("top_ready")
        l_ready = sem("l_ready")
        lexp_ready = sem("lexp_ready")
        rw_ready = sem("rw_ready")
        mx_done = sem("mx_done")
        q_ready = sem("q_ready")
        sum_ready = sem("sum_ready")
        sc_step = sem("sc_step")
        sc_ready = sem("sc_ready")
        w1h_ready = sem("w1h_ready")
        w1l_ready = sem("w1l_ready")
        w2h_ready = sem("w2h_ready")
        w2l_ready = sem("w2l_ready")
        up_mm = sem("up_mm")
        g_ready = sem("g_ready")
        hh_ready = sem("hh_ready")
        hl_ready = sem("hl_ready")
        down_mm = sem("down_mm")
        b2_step = sem("b2_step")
        b2_done = sem("b2_done")
        acc_done = sem("acc_done")

        block = ctx.enter_context(nc.Block())

        pe_engine = nc.tensor

        def walk_groups(stage):
            stage(0, None, 1)
            for g in range(1, NG - 1):
                stage(g, g - 1, g + 1)
            stage(NG - 1, NG - 2, None)
            stage(None, NG - 1, None)

        def walk_chunks(eng, up, down, early, prepare):
            def pair(c, last):
                for par in range(2):
                    more = not (last and par == 1)
                    if more:
                        early(c + par + 1, 1 - par)
                    up(c + par, par, 1)
                    down(c + par, par, 0)
                    if more:
                        prepare(c + par + 1, 1 - par)
                    if eng is pe_engine:
                        with eng.Fori(1, NB - 1) as n:
                            up(c + par, par, n + 1)
                            down(c + par, par, n)
                    else:
                        for n in range(1, NB - 1):
                            up(c + par, par, n + 1)
                            down(c + par, par, n)
                    if more:
                        up(c + par + 1, 1 - par, 0)
                    down(c + par, par, NB - 1)

            early(0, 0)
            prepare(0, 0)
            up(0, 0, 0)
            with eng.Fori(0, NCH // 2 - 1) as i:
                pair(2 * i, False)
            pair(NCH - 2, True)

        @block.sync
        def _(sp):
            for g in range(NG):
                sp.dma_start(xa[:, g * GB:(g + 1) * GB, :], x_v[:, g * GB:(g + 1) * GB, :]).then_inc(d_x[g], 16)
                sp.dma_start(vn[:, g * GB:(g + 1) * GB, :], v_v[:, g * GB:(g + 1) * GB, :]).then_inc(d_v[g], 16)
            for g in range(NG):
                sp.wait_ge(d_x[g], 16)
                sp.sem_inc(x_landed, 1)
                sp.wait_ge(d_v[g], 16)
                sp.sem_inc(v_landed, 1)

            sp.wait_ge(top_ready, 1)
            picked = [sp.value_load(topi[0:1, k:k + 1], min_val=0, max_val=E - 1) for k in range(TOPK)]

            def load_chunk(k, j, c):
                wait(sp, w1h_ready, c)
                wait(sp, w1l_ready, c)
                sp.dma_start(stage1[:, :, :],
                             w1[bass.ds(picked[k], 1), :, bass.ds(j * FC, FC)]
                             .rearrange("e (k p) f -> p (e k) f", p=P)).then_inc(d_w1, 16)
                wait(sp, w2h_ready, c)
                wait(sp, w2l_ready, c)
                sp.dma_start(stage2[:, :, :],
                             w2[bass.ds(picked[k], 1), bass.ds(j * FC, FC), :]
                             .rearrange("e (k p) d -> p (e k) d", p=P)).then_inc(d_w2, 16)

            load_chunk(0, 0, 0)
            for k in range(TOPK):
                sp.dma_start(b2b[:, k, :], b2[bass.ds(picked[k], 1), :].broadcast_to([P, C])).then_inc(d_b2, 16)
            with sp.Fori(1, CPE) as j:
                load_chunk(0, j, j)
            with sp.Fori(0, CPE) as j:
                load_chunk(1, j, j + CPE)
            with sp.Fori(0, TILES) as t:
                sp.wait_ge(acc_done, t + NCH * TILES + 1)
                sp.dma_start(out_v[:, bass.ds(t, 1), :], xa[:, bass.ds(t, 1), :]).then_inc(d_out, 16)
            sp.wait_ge(d_out, 16 * TILES)

        @block.gpsimd
        def _(pool):
            nc.gpsimd.memset(ident[:, :], 0.0).then_inc(c_pool, 1)
            pool.wait_ge(c_pool, 1)
            nc.gpsimd.affine_select(out=ident[:, :], in_=ident[:, :], compare_op=ALU.not_equal, fill=1.0,
                                    base=0, pattern=[[-1, P]], channel_multiplier=1).then_inc(c_id, 1)
            nc.gpsimd.memset(ones[:, :], 1.0).then_inc(c_pool, 1)
            nc.gpsimd.memset(eps[:, :], LN_EPS).then_inc(c_pool, 1)
            nc.gpsimd.memset(mask[:, :], 1.0).then_inc(c_pool, 1)
            pool.wait_ge(c_pool, 4)
            nc.gpsimd.memset(mask[:, :].rearrange("p (b n) -> p b n", n=SEG)[:, :, 0:2], 0.0).then_inc(c_pool, 1)
            nc.gpsimd.memset(s1.rearrange("p k (b n) -> p (k b) n", n=SEG)[:, :, 0:1], 1.0).then_inc(c_pool, 1)
            for e in range(E):
                nc.gpsimd.memset(iota[:, e:e + 1], float(e)).then_inc(c_pool, 1)

            def shifted(buf, j):
                return buf[:, j, :].rearrange("p (b n) -> p b n", n=SEG)[:, :, 0:T]

            def stage(front, back, ahead):
                if front is None:
                    return

                def sums(j):
                    u = front * CT + j
                    pool.wait_ge(sv_ready, u + 1)
                    num = ekv[:, j, :].rearrange("p (b n) -> p b n", n=T)
                    nc.gpsimd.tensor_tensor(num, num, shifted(sv, j), ALU.add).then_inc(num_done, 1)
                    pool.wait_ge(s1_ready, u + 1)
                    den = ek[:, j, :].rearrange("p (b n) -> p b n", n=T)
                    nc.gpsimd.tensor_tensor(den, den, shifted(s1, j), ALU.add).then_inc(den_done, 1)

                def ratio(j):
                    u = front * CT + j
                    pool.wait_ge(r_ready, u + 1)
                    pool.wait_ge(num_done, u + 1)
                    if j == 0:
                        pool.wait_ge(kT_ready, front * CT + CT)
                    nc.gpsimd.tensor_tensor(yT[:, front_at, j, :], ekv[:, j, :], ek[:, j, :],
                                            ALU.mult).then_inc(y_done, 1)

                front_at = front
                sums(0)
                sums(1)
                ratio(0)
                sums(2)
                ratio(1)
                sums(3)
                ratio(2)
                ratio(3)

            walk_groups(stage)

            pool.wait_ge(rw_ready, 1)
            pool.wait_ge(d_b2, 16 * TOPK)
            with pool.Fori(0, TILES) as t:
                for k in range(TOPK):
                    nc.gpsimd.tensor_tensor(bt[:, k, :], b2b[:, k, :], rw[:, k, bass.ds(t, 1)].broadcast_to([P, C]),
                                            ALU.mult).then_inc(b2_step, 1)
                pool.wait_ge(b2_step, t * 3 + 2)
                nc.gpsimd.tensor_tensor(bt[:, 0, :], bt[:, 0, :], bt[:, 1, :], ALU.add).then_inc(b2_step, 1)
                pool.wait_ge(b2_step, t * 3 + 3)
                xt = xa[:, bass.ds(t, 1), :].rearrange("p a c -> p (a c)")
                nc.gpsimd.tensor_tensor(xt, xt, bt[:, 0, :], ALU.add).then_inc(b2_done, 1)
                pool.wait_ge(b2_done, t + 1)

        @block.scalar
        def _(act):
            nc.scalar.preload_act_table_set("natural_log_exp_and_others")
            act.dma_start(rows[0:CT, :], time_decay.rearrange("(k p) -> k p", p=P)).then_inc(d_rows, 16)
            act.dma_start(rows[CT:2 * CT, :], time_first.rearrange("(k p) -> k p", p=P)).then_inc(d_rows, 16)
            act.dma_start(gate_rows[:, :], gate_w).then_inc(d_rows, 16)
            act.dma_start(b1rows[:, :], b1.rearrange("e (k p) -> (e k) p", p=P)).then_inc(d_rows, 16)
            act.wait_ge(c_cols, 1)
            nc.scalar.activation(edec[:, :], cols[:, 0:CT], ACT.Exp).then_inc(c_edec, 1)
            act.wait_ge(c_edec, 1)
            nc.scalar.activation(dcol[:, :], edec[:, :], ACT.Exp, scale=-1.0).then_inc(c_dcol, 1)
            act.wait_ge(c_pool, 6 + E)
            act.wait_ge(c_dve, 2)

            def normalise(g):
                act.wait_ge(mv_ready, g * GB + GB)
                nc.scalar.activation(lnv[:, bass.ds(g * GB, GB)], mv[:, bass.ds(g * GB, GB), 1],
                                     ACT.Ln, bias=eps[:, 0:1]).then_inc(lnv_done, 1)
                act.wait_ge(lnv_done, g + 1)
                nc.scalar.activation(rstd[:, bass.ds(g * GB, GB)], lnv[:, bass.ds(g * GB, GB)],
                                     ACT.Exp, scale=-0.5).then_inc(rstd_ready, 1)
                act.wait_ge(nmr_ready, g + 1)
                for j in range(GB):
                    t = g * GB + j
                    nc.scalar.activation(kn[:, bass.ds(g, 1), j, :].rearrange("p a c -> p (a c)"),
                                         xa[:, bass.ds(t, 1), :].rearrange("p a c -> p (a c)"), ACT.Identity,
                                         scale=rstd[:, bass.ds(t, 1)], bias=nmr[:, bass.ds(t, 1)]).then_inc(kn_ready, 1)

            def stage(front, back, ahead):
                def keys(j):
                    u = front * CT + j
                    act.wait_ge(kT_ready, u + 1)
                    wait(act, y_done, u - CT + 1)
                    nc.scalar.activation(ek[:, j, :], psK[j % 2], ACT.Exp, bias=um[:, j:j + 1]).then_inc(ek_ready, 1)
                    nc.scalar.activation(s1[:, j, :].rearrange("p (b n) -> p b n", n=SEG)[:, :, 1:SEG],
                                         psK[j % 2].rearrange("p (b n) -> p b n", n=T), ACT.Exp,
                                         bias=nup[:, j:j + 1]).then_inc(keys_ready, 1)

                def inverse(j):
                    u = front * CT + j
                    act.wait_ge(den_done, u + 1)
                    nc.scalar.activation(ek[:, j, :], ek[:, j, :], ACT.Ln).then_inc(lnd_done, 1)
                    act.wait_ge(lnd_done, u + 1)
                    nc.scalar.activation(ek[:, j, :], ek[:, j, :], ACT.Exp, scale=-1.0).then_inc(r_ready, 1)

                def variance(j):
                    t = back * GB + j
                    act.wait_ge(nm_ready, t + 1)
                    wait(act, sq_done, t)
                    nc.scalar.activation(junk, xa[:, bass.ds(t, 1), :].rearrange("p a c -> p (a c)"), ACT.Square,
                                         bias=nm[:, bass.ds(t, 1)], accum_out=ssq[:, bass.ds(t, 1)]).then_inc(sq_done, 1)
                    act.wait_ge(sq_done, t + 1)
                    nc.scalar.activation(lnv2[:, bass.ds(t, 1)], ssq[:, bass.ds(t, 1)], ACT.Ln,
                                         bias=eps[:, 0:1], scale=1.0 / C).then_inc(lnv2_done, 1)
                    act.wait_ge(lnv2_done, t + 1)
                    nc.scalar.activation(rs2[:, bass.ds(t, 1)], lnv2[:, bass.ds(t, 1)], ACT.Exp,
                                         scale=-0.5).then_inc(rs2_ready, 1)

                def high(j):
                    t = back * GB + j
                    act.wait_ge(x2T_ready, t + 1)
                    nc.scalar.activation(xh[:, :, bass.ds(t * P, P)],
                                         psX[j % 2].rearrange("p (k n) -> p k n", k=CT),
                                         ACT.Copy, scale=X_SCALE).then_inc(xh_ready, 1)

                f, b = front is not None, back is not None
                if f:
                    keys(0)
                    keys(1)
                if b:
                    variance(0)
                if f:
                    keys(2)
                    inverse(0)
                if b:
                    variance(1)
                    high(0)
                if f:
                    keys(3)
                    inverse(1)
                if b:
                    variance(2)
                    high(1)
                if f:
                    inverse(2)
                if ahead is not None:
                    normalise(ahead)
                if b:
                    variance(3)
                    high(2)
                if f:
                    inverse(3)
                if b:
                    high(3)

            normalise(0)
            walk_groups(stage)

            act.wait_ge(l_ready, 1)
            nc.scalar.activation(lexp[:, :, :], lsel[:, :, :], ACT.Exp, scale=1.0 / X_SCALE).then_inc(lexp_ready, 1)
            nc.scalar.preload_act_table(ACT.Gelu_apprx_tanh)

            def early(c, par):
                pass

            def prepare(c, par):
                act.wait_ge(sc_ready, c + 1)
                wait(act, up_mm, (c - 1) * NB * FT)
                nc.scalar.activation(w1h[:, par, :, :], stage1[:, :, :], ACT.Identity,
                                     scale=scale[:, par, 0:1]).then_inc(w1h_ready, 1)
                wait(act, down_mm, c * TILES)
                nc.scalar.activation(w2h[:, par, :, :], stage2[:, :, :], ACT.Identity,
                                     scale=scale[:, par, 1:2]).then_inc(w2h_ready, 1)

            def up(c, par, n):
                for f in range(FT):
                    u = c * (NB * FT) + n * FT + f
                    act.wait_ge(up_mm, u + 1)
                    wait(act, hl_ready, u - FT + 1)
                    nc.scalar.activation(g32[:, f, :], psA[f], ACT.Gelu_apprx_tanh,
                                         scale=gsc[:, par:par + 1],
                                         bias=bias[:, par, f:f + 1]).then_inc(g_ready, 1)
                    act.wait_ge(g_ready, u + 1)
                    act.wait_ge(down_mm, c * TILES + n * GB + GB)
                    nc.scalar.activation(hh[:, bass.ds(n, 1), f, :].rearrange("p a t -> p (a t)"), g32[:, f, :],
                                         ACT.Identity, scale=scale[:, par, 2:3]).then_inc(hh_ready, 1)

            walk_chunks(act, up, lambda c, par, n: None, early, prepare)

        @block.vector
        def _(dve):
            dve.wait_ge(c_gateT, 1)
            nc.vector.tensor_copy(cols[:, :], psM[:, 0:2 * CT]).then_inc(c_cols, 1)
            dve.wait_ge(c_cols, 1)
            nc.vector.tensor_scalar(um[:, :], cols[:, CT:2 * CT], 0.0, None, ALU.min).then_inc(c_dve, 1)
            nc.vector.tensor_scalar(nup[:, :], cols[:, CT:2 * CT], 0.0, -1.0, ALU.max, ALU.mult).then_inc(c_dve, 1)
            dve.wait_ge(c_pool, 6 + E)

            def statistics(g, tiles):
                for j in tiles:
                    t = g * GB + j
                    wait(dve, mv_ready, t - GB + 1)
                    nc.vector.bn_stats(bn[:, j, :], xa[:, bass.ds(t, 1), :].rearrange("p a c -> p (a c)")).then_inc(bn_done, 1)
                for j in tiles:
                    t = g * GB + j
                    dve.wait_ge(bn_done, t + 1)
                    nc.vector.bn_aggr(mv[:, bass.ds(t, 1), :].rearrange("p a c -> p (a c)"), bn[:, j, :]).then_inc(mv_ready, 1)

            def minus_mean(g):
                dve.wait_ge(rstd_ready, g + 1)
                nc.vector.scalar_tensor_tensor(nmr[:, bass.ds(g * GB, GB)], mv[:, bass.ds(g * GB, GB), 0], -1.0,
                                               rstd[:, bass.ds(g * GB, GB)], ALU.mult, ALU.mult).then_inc(nmr_ready, 1)

            dve.wait_ge(x_landed, 1)
            statistics(0, range(GB))
            minus_mean(0)
            dve.wait_ge(c_dcol, 1)
            for j in range(CT):
                nc.vector.tensor_scalar(decay[:, j, :], mask[:, :], dcol[:, j:j + 1], None, ALU.mult).then_inc(c_dve, 1)
            gsrc = psM[:, 64:64 + CT * E].rearrange("p (k e) -> p k e", k=CT)
            nc.vector.tensor_copy(gT[:, :, :], gsrc).then_inc(c_g3, 1)
            nc.vector.tensor_copy(b1T[:, :, :].rearrange("p e f -> p (e f)"), psM[:, 128:256]).then_inc(c_ready, 1)
            dve.wait_ge(c_g3, 1)
            nc.vector.tensor_copy(g3[:, :, 0, :], gT[:, :, :]).then_inc(c_g3, 1)
            dve.wait_ge(c_g3, 2)
            nc.vector.tensor_tensor(gres[:, 0, :, :], gT[:, :, :], g3[:, :, 0, :], ALU.subtract).then_inc(c_g3, 1)
            dve.wait_ge(c_g3, 3)
            nc.vector.tensor_copy(g3[:, :, 1, :], gres[:, 0, :, :]).then_inc(c_g3, 1)
            dve.wait_ge(c_g3, 4)
            nc.vector.tensor_tensor(gres[:, 1, :, :], gres[:, 0, :, :], g3[:, :, 1, :], ALU.subtract).then_inc(c_g3, 1)
            dve.wait_ge(c_g3, 5)
            nc.vector.tensor_copy(g3[:, :, 2, :], gres[:, 1, :, :]).then_inc(c_g3, 1)
            dve.wait_ge(c_dve, 2 + CT)

            def stage(front, back, ahead):
                def states(j):
                    u = front * CT + j
                    dve.wait_ge(keys_ready, u + 1)
                    dve.wait_ge(vT_ready, u + 1)
                    vt = psV[j % 2].rearrange("p (b n) -> p b n", n=T)
                    sv3 = sv[:, j, :].rearrange("p (b n) -> p b n", n=SEG)
                    s13 = s1[:, j, :].rearrange("p (b n) -> p b n", n=SEG)
                    nc.vector.tensor_copy(sv3[:, :, 0], vt[:, :, 0]).then_inc(sv_in, 1)
                    nc.vector.tensor_tensor(sv3[:, :, 1:SEG], s13[:, :, 1:SEG], vt, ALU.mult).then_inc(sv_in, 1)
                    nc.vector.tensor_tensor(ekv[:, j, :], ek[:, j, :], psV[j % 2], ALU.mult).then_inc(v_used, 1)
                    dve.wait_ge(sv_in, 2 * u + 2)
                    nc.vector.tensor_tensor_scan(sv[:, j, :], decay[:, j, :], sv[:, j, :], 0.0,
                                                 ALU.mult, ALU.add).then_inc(sv_ready, 1)
                    nc.vector.tensor_tensor_scan(s1[:, j, :], decay[:, j, :], s1[:, j, :], 0.0,
                                                 ALU.mult, ALU.add).then_inc(s1_ready, 1)

                def residual(j):
                    t = back * GB + j
                    dve.wait_ge(yT_ready, t + 1)
                    xt = xa[:, bass.ds(t, 1), :].rearrange("p a c -> p (a c)")
                    nc.vector.scalar_tensor_tensor(xt, psY, 1.0, xt, ALU.mult, ALU.add,
                                                   accum_out=sm[:, bass.ds(t, 1)]).then_inc(x1_ready, 1)
                    dve.wait_ge(x1_ready, t + 1)
                    nc.vector.tensor_scalar(nm[:, bass.ds(t, 1)], sm[:, bass.ds(t, 1)], -1.0 / C, None,
                                            ALU.mult).then_inc(nm_ready, 1)

                def second_norm(j):
                    t = back * GB + j
                    dve.wait_ge(rs2_ready, t + 1)
                    wait(dve, x2T_ready, t - 1)
                    nc.vector.tensor_scalar(x2n[:, j % 2, :], xa[:, bass.ds(t, 1), :].rearrange("p a c -> p (a c)"),
                                            nm[:, bass.ds(t, 1)], rs2[:, bass.ds(t, 1)],
                                            ALU.add, ALU.mult).then_inc(x2n_ready, 1)

                def low(j):
                    t = back * GB + j
                    dve.wait_ge(xh_ready, t + 1)
                    nc.vector.scalar_tensor_tensor(xl[:, :, bass.ds(t * P, P)],
                                                   psX[j % 2].rearrange("p (k n) -> p k n", k=CT), X_SCALE,
                                                   xh[:, :, bass.ds(t * P, P)], ALU.mult, ALU.subtract).then_inc(xl_ready, 1)

                def logit(j):
                    t = back * GB + j
                    dve.wait_ge(lg_mm, t + 1)
                    nc.vector.tensor_reduce(logits[:, bass.ds(t, 1), :].rearrange("p a e -> p (a e)"),
                                            psM[:, 0:3 * E].rearrange("p (s e) -> p e s", s=3), AX_X,
                                            ALU.add).then_inc(lg_done, 1)

                f, b = front is not None, back is not None
                if f:
                    states(0)
                if b:
                    residual(0)
                if f:
                    states(1)
                if ahead is not None:
                    dve.wait_ge(x_landed, ahead + 1)
                    statistics(ahead, (0, 1))
                if b:
                    residual(1)
                    second_norm(0)
                if f:
                    states(2)
                if ahead is not None:
                    statistics(ahead, (2, 3))
                if b:
                    residual(2)
                    low(0)
                    second_norm(1)
                if f:
                    states(3)
                if ahead is not None:
                    minus_mean(ahead)
                if b:
                    residual(3)
                    logit(0)
                    low(1)
                    second_norm(2)
                    logit(1)
                    low(2)
                    second_norm(3)
                    logit(2)
                    low(3)
                    logit(3)

            walk_groups(stage)

            step = [0]

            def link(ins):
                step[0] += 1
                ins.then_inc(rt, 1)
                dve.wait_ge(rt, step[0])

            dve.wait_ge(tot_mm, 1)
            link(nc.vector.tensor_reduce(tot[:, :], psM[:, 128:128 + TILES * E].rearrange("p (t e) -> p e t", e=E),
                                         AX_X, ALU.add))
            link(nc.vector.max(top[:, :], tot[:, :]))
            nc.vector.max_index(topi[:, :], top[:, :], tot[:, :]).then_inc(top_ready, 1)
            dve.wait_ge(top_ready, 1)
            link(nc.vector.tensor_copy(topf[:, :], topi[:, :]))
            for k in range(TOPK):
                link(nc.vector.tensor_scalar(pick[:, k, :], iota[:, :], topf[:, k:k + 1], None, ALU.is_equal))
            for k in range(TOPK):
                link(nc.vector.tensor_tensor(b1tmp[:, :, :], b1T[:, :, :].rearrange("p e f -> p f e"),
                                             pick[:, k:k + 1, :].broadcast_to([P, DFF // P, E]), ALU.mult))
                link(nc.vector.tensor_reduce(b1c[:, k, :], b1tmp[:, :, :], AX_X, ALU.add))
                link(nc.vector.tensor_reduce(mb[:, k:k + 1], b1c[:, k, :], AX_X, ALU.max, apply_absolute_value=True))
                link(nc.vector.tensor_tensor(mb[:, k:k + 1], mb[:, k:k + 1], mb[:, k:k + 1], ALU.mult))
                link(nc.vector.tensor_scalar(mb2[:, k * CPE:(k + 1) * CPE], mb[:, k:k + 1].broadcast_to([P, CPE]),
                                             2.0, None, ALU.mult))
                link(nc.vector.tensor_tensor(ptmp[:, :, :], logits[:, :, :],
                                             pick[:, k:k + 1, :].broadcast_to([P, TILES, E]), ALU.mult))
                link(nc.vector.tensor_reduce(lsel[:, k, :], ptmp[:, :, :], AX_X, ALU.add))
            link(nc.vector.tensor_tensor(lmax[:, :], lsel[:, 0, :], lsel[:, 1, :], ALU.max))
            link(nc.vector.tensor_tensor(lsel[:, 0, :], lsel[:, 0, :], lmax[:, :], ALU.subtract))
            nc.vector.tensor_tensor(lsel[:, 1, :], lsel[:, 1, :], lmax[:, :], ALU.subtract).then_inc(l_ready, 1)
            dve.wait_ge(lexp_ready, 1)
            link(nc.vector.tensor_tensor(lsum[:, :], lexp[:, 0, :], lexp[:, 1, :], ALU.add))
            link(nc.vector.reciprocal(linv[:, :], lsum[:, :]))
            link(nc.vector.tensor_tensor(rw[:, 0, :], lexp[:, 0, :], linv[:, :], ALU.mult))
            nc.vector.tensor_tensor(rw[:, 1, :], lexp[:, 1, :], linv[:, :], ALU.mult).then_inc(rw_ready, 1)
            dve.wait_ge(rw_ready, 1)
            for k in range(TOPK):
                for c in range(k * CPE, (k + 1) * CPE):
                    nc.vector.tensor_copy(rwd[:, c, :], rw[:, k, :]).then_inc(rt, 1)
                    step[0] += 1
            dve.wait_ge(rt, step[0])

            def early(c, par):
                dve.wait_ge(d_w1, c * 16 + 16)
                nc.vector.tensor_reduce(mx[:, bass.ds(c, 1), 0], stage1[:, :, :], AX_XY, ALU.max,
                                        apply_absolute_value=True).then_inc(mx_done, 1)
                dve.wait_ge(d_w2, c * 16 + 16)
                nc.vector.tensor_reduce(mx[:, bass.ds(c, 1), 1], stage2[:, :, :], AX_XY, ALU.max,
                                        apply_absolute_value=True).then_inc(mx_done, 1)
                dve.wait_ge(mx_done, c * 3 + 2)
                mc = mx[:, bass.ds(c, 1), :].rearrange("p a c -> p (a c)")
                nc.vector.tensor_tensor(q[:, bass.ds(c, 1), 0:2].rearrange("p a c -> p (a c)"), mc, mc,
                                        ALU.mult).then_inc(mx_done, 1)
                dve.wait_ge(mx_done, c * 3 + 3)
                nc.vector.scalar_tensor_tensor(q[:, bass.ds(c, 1), 2], q[:, bass.ds(c, 1), 0], 2.0 * C * CT,
                                               mb2[:, bass.ds(c, 1)], ALU.mult, ALU.add).then_inc(q_ready, 1)

            def prepare(c, par):
                def row(buf):
                    return buf[:, par, :]

                def small(k, ins):
                    ins.then_inc(sc_step, 1)
                    dve.wait_ge(sc_step, c * SMALL + k)

                SMALL = 9
                dve.wait_ge(sum_ready, c + 1)
                wait(dve, g_ready, c * NB * FT - NB * FT)
                wait(dve, hl_ready, c * NB * FT - NB * FT)
                nc.vector.tensor_copy(bias[:, par, :], b1c[:, :, :].rearrange("p k f -> p (k f)")
                                      [:, bass.ds(c * FT, FT)]).then_inc(sc_step, 1)
                small(2, nc.vector.tensor_scalar(row(eb), psS.bitcast(I32), 23, None, ALU.logical_shift_right))
                small(3, nc.vector.tensor_scalar(row(eh), row(eb), 129.0, None, ALU.add))
                small(4, nc.vector.tensor_scalar(row(eb), row(eh), 1, None, ALU.logical_shift_right))
                small(5, nc.vector.tensor_scalar(row(ei), row(eb), -1.0, 268.0, ALU.mult, ALU.add))
                small(6, nc.vector.tensor_scalar(row(scale).bitcast(I32), row(ei), 23, None, ALU.logical_shift_left))
                small(7, nc.vector.tensor_scalar(row(eh), row(eb), -14.0, None, ALU.add))
                small(8, nc.vector.tensor_scalar(row(descale).bitcast(I32), row(eh), 23, None, ALU.logical_shift_left))
                rc = rwd[:, bass.ds(c, 1), :].rearrange("p a c -> p (a c)")
                small(9, nc.vector.tensor_scalar(rc, rc, descale[:, par, 1:2], descale[:, par, 2:3],
                                                 ALU.mult, ALU.mult))
                nc.vector.tensor_scalar(gsc[:, par:par + 1], descale[:, par, 0:1], 1.0 / X_SCALE, None,
                                        ALU.mult).then_inc(sc_ready, 1)
                dve.wait_ge(w1h_ready, c + 1)
                nc.vector.scalar_tensor_tensor(w1l[:, par, :, :], stage1[:, :, :], scale[:, par, 0:1],
                                               w1h[:, par, :, :], ALU.mult, ALU.subtract).then_inc(w1l_ready, 1)
                dve.wait_ge(w2h_ready, c + 1)
                nc.vector.scalar_tensor_tensor(w2l[:, par, :, :], stage2[:, :, :], scale[:, par, 1:2],
                                               w2h[:, par, :, :], ALU.mult, ALU.subtract).then_inc(w2l_ready, 1)

            def up(c, par, n):
                for f in range(FT):
                    dve.wait_ge(hh_ready, c * (NB * FT) + n * FT + f + 1)
                    nc.vector.scalar_tensor_tensor(hl[:, bass.ds(n, 1), f, :].rearrange("p a t -> p (a t)"),
                                                   g32[:, f, :], scale[:, par, 2:3],
                                                   hh[:, bass.ds(n, 1), f, :].rearrange("p a t -> p (a t)"),
                                                   ALU.mult, ALU.subtract).then_inc(hl_ready, 1)

            def down(c, par, n):
                for t in range(GB):
                    tile = n * GB + t
                    dve.wait_ge(down_mm, (c + 1) * TILES + tile + 1)
                    dve.wait_ge(b2_done, tile + 1)
                    dve.wait_ge(acc_done, c * TILES + tile + 1)
                    xt = xa[:, bass.ds(tile, 1), :].rearrange("p a c -> p (a c)")
                    nc.vector.scalar_tensor_tensor(xt, psB[t % 2],
                                                   rwd[:, bass.ds(c, 1), bass.ds(tile, 1)].rearrange("p a c -> p (a c)"),
                                                   xt, ALU.mult, ALU.add).then_inc(acc_done, 1)

            dve.sem_inc(acc_done, TILES)
            walk_chunks(dve, up, down, early, prepare)

        @block.tensor
        def _(pe):
            pe.wait_ge(c_id, 1)
            pe.wait_ge(d_rows, 64)
            nc.tensor.transpose(psM[:, 0:2 * CT], rows[0:2 * CT, :], ident[0:2 * CT, 0:2 * CT])
            for k in range(CT):
                nc.tensor.transpose(psM[:, 64 + k * E:64 + (k + 1) * E], gate_rows[:, k * P:(k + 1) * P],
                                    ident[0:E, 0:E])
            nc.tensor.transpose(psM[:, 128:256], b1rows[:, :], ident[:, :]).then_inc(c_gateT, 1)

            def stage(front, back, ahead):
                def turn(j):
                    u = front * CT + j
                    if j == 0:
                        pe.wait_ge(kn_ready, front * GB + GB)
                        pe.wait_ge(v_landed, front + 1)
                    wait(pe, keys_ready, u - 1)
                    for t in range(GB):
                        last = nc.tensor.transpose(psK[j % 2][:, t * P:(t + 1) * P],
                                                   kn[:, bass.ds(front, 1), t, j * P:(j + 1) * P]
                                                   .rearrange("p a c -> p (a c)"), ident[:, :])
                    last.then_inc(kT_ready, 1)
                    wait(pe, v_used, u - 1)
                    for t in range(GB):
                        last = nc.tensor.transpose(psV[j % 2][:, t * P:(t + 1) * P],
                                                   vn[:, bass.ds(front * GB + t, 1), j * P:(j + 1) * P]
                                                   .rearrange("p a c -> p (a c)"), ident[:, :])
                    last.then_inc(vT_ready, 1)

                def turn_y(j):
                    t = back * GB + j
                    if j == 0:
                        pe.wait_ge(y_done, back * CT + CT)
                    wait(pe, x1_ready, t)
                    for k in range(CT):
                        last = nc.tensor.transpose(psY[:, k * P:(k + 1) * P],
                                                   yT[:, bass.ds(back, 1), k, j * P:(j + 1) * P]
                                                   .rearrange("p a n -> p (a n)"), ident[:, :])
                    last.then_inc(yT_ready, 1)

                def turn_x(j):
                    t = back * GB + j
                    pe.wait_ge(x2n_ready, t + 1)
                    wait(pe, xl_ready, t - 1)
                    for k in range(CT):
                        last = nc.tensor.transpose(psX[j % 2][:, k * P:(k + 1) * P], x2n[:, j % 2, k * P:(k + 1) * P],
                                                   ident[:, :])
                    last.then_inc(x2T_ready, 1)

                def router(j):
                    t = back * GB + j
                    pe.wait_ge(xl_ready, t + 1)
                    if j == 0:
                        pe.wait_ge(c_g3, 6)
                        pe.wait_ge(c_ready, 1)
                    wait(pe, lg_done, t)
                    for n, part in enumerate((xh, xl)):
                        for k in range(CT):
                            last = nc.tensor.matmul(psM[:, 0:3 * E], part[:, k, bass.ds(t * P, P)],
                                                    g3[:, k, :, :].rearrange("p s e -> p (s e)"),
                                                    start=(n == 0 and k == 0), stop=(n == 1 and k == CT - 1))
                    last.then_inc(lg_mm, 1)

                f, b = front is not None, back is not None
                if f:
                    turn(0)
                if b:
                    turn_y(0)
                if f:
                    turn(1)
                if b:
                    turn_y(1)
                if f:
                    turn(2)
                if b:
                    turn_x(0)
                    turn_y(2)
                if f:
                    turn(3)
                if b:
                    turn_x(1)
                    turn_y(3)
                    router(0)
                    turn_x(2)
                    router(1)
                    turn_x(3)
                    router(2)
                    router(3)

            walk_groups(stage)

            pe.wait_ge(lg_done, TILES)
            nc.tensor.matmul(psM[:, 128:128 + TILES * E], ones[:, :], logits[:, :, :].rearrange("p t e -> p (t e)"),
                             start=True, stop=True).then_inc(tot_mm, 1)

            def early(c, par):
                pass

            def prepare(c, par):
                pe.wait_ge(q_ready, c + 1)
                nc.tensor.matmul(psS, ones[:, :], q[:, bass.ds(c, 1), :].rearrange("p a c -> p (a c)"),
                                 start=True, stop=True).then_inc(sum_ready, 1)

            def up(c, par, n):
                if isinstance(n, int) and n == 0:
                    pe.wait_ge(w1l_ready, c + 1)
                def tokens(part, k):
                    return part[:, k, bass.ds(n * GT, GT)]
                for f in range(FT):
                    wait(pe, g_ready, c * (NB * FT) + n * FT + f - FT + 1)
                    for k in range(CT):
                        a_h = w1h[:, par, k, f * P:(f + 1) * P]
                        a_l = w1l[:, par, k, f * P:(f + 1) * P]
                        nc.tensor.matmul(psA[f], a_h, tokens(xh, k), start=(k == 0), stop=False)
                        nc.tensor.matmul(psA[f], a_h, tokens(xl, k), start=False, stop=False)
                        last = nc.tensor.matmul(psA[f], a_l, tokens(xh, k), start=False, stop=(k == CT - 1))
                    last.then_inc(up_mm, 1)

            def down(c, par, n):
                if isinstance(n, int) and n == 0:
                    pe.wait_ge(w2l_ready, c + 1)
                pe.wait_ge(hl_ready, c * (NB * FT) + n * FT + FT)
                for t in range(GB):
                    pe.wait_ge(acc_done, (c + 1) * TILES + n * GB + t - 1)
                    for f in range(FT):
                        hid_h = hh[:, bass.ds(n, 1), f, t * P:(t + 1) * P].rearrange("p a t -> p (a t)")
                        hid_l = hl[:, bass.ds(n, 1), f, t * P:(t + 1) * P].rearrange("p a t -> p (a t)")
                        nc.tensor.matmul(psB[t % 2], hid_h, w2h[:, par, f, :], start=(f == 0), stop=False)
                        nc.tensor.matmul(psB[t % 2], hid_h, w2l[:, par, f, :], start=False, stop=False)
                        last = nc.tensor.matmul(psB[t % 2], hid_l, w2h[:, par, f, :], start=False, stop=(f == FT - 1))
                    last.then_inc(down_mm, 1)

            pe.sem_inc(down_mm, TILES)
            walk_chunks(pe, up, down, early, prepare)


_INS = ['x', 'ctx_2048', 'L0_xattn_time_decay', 'L0_xattn_time_first', 'L0_ffn_gate_w', 'L0_ffn_w1', 'L0_ffn_b1',
        'L0_ffn_w2', 'L0_ffn_b2']
_OUTS = [((8, 256, 512), 'float32')]


def kernel(**inputs):
    import numpy as _np
    import concourse.bacc as _bacc
    from concourse import mybir as _mybir
    from concourse.bass_utils import run_bass_kernel_spmd as _run

    nc = _bacc.Bacc("TRN2", target_bir_lowering=False, num_devices=1)
    arrays, args = {}, []
    for name in _INS:
        a = _np.ascontiguousarray(inputs[name])
        arrays[f"in_{name}_dram"] = a
        args.append(nc.dram_tensor(f"in_{name}_dram", a.shape, _mybir.dt.from_np(a.dtype), kind="ExternalInput").ap())
    for i, (shape, dtype) in enumerate(_OUTS):
        dt = _mybir.dt.from_np(_np.dtype(dtype))
        args.append(nc.dram_tensor(f"out_{i}_dram", shape, dt, kind="ExternalOutput").ap())
    wkv_moe_kernel(nc, *args)
    r = _run(nc, [arrays], core_ids=[0])
    return r.results[0]["out_0_dram"]
```

```python
from contextlib import ExitStack

import concourse.bass as bass
from concourse import mybir

P = 128
F32 = mybir.dt.float32
F16 = mybir.dt.float16
BF16 = mybir.dt.bfloat16
I32 = mybir.dt.int32
U32 = mybir.dt.uint32
ALU = mybir.AluOpType
ACT = mybir.ActivationFunctionType
AX_X = mybir.AxisListType.X
AX_XY = mybir.AxisListType.XY

LN_EPS = 1e-5
LAG_STATES = 1
LAG_INVERSE = 2
LAG_RATIO = 3
LAG_TURN_Y = 6
LAG_RESIDUAL = 7
LAG_NORM = 8
LAG_SPLIT = 9
LAG_LOGIT = 10
X_SCALE = 1024.0


def wait(eng, sem, value):
    if not (isinstance(value, int) and value <= 0):
        eng.wait_ge(sem, value)


def wkv_moe_kernel(nc, x, ctx_in, time_decay, time_first, gate_w, w1, b1, w2, b2, out):
    B, T, C = x.shape
    E, _, DFF = w1.shape
    TOPK = 2
    N = B * T
    TILES = N // P
    CT = C // P
    GB = 4
    GT = GB * P
    NG = TILES // GB
    RB = GT // T
    SEG = T + 1
    FC = 512
    FT = FC // P
    CPE = DFF // FC
    NCH = TOPK * CPE
    NB = N // GT
    assert NB == 4 and FT == 4 and CT == 4 and GB == 4 and C == 512 and NCH % 2 == 0

    x_v = x.rearrange("b t c -> (b t) c").rearrange("(n p) c -> p n c", p=P)
    v_v = ctx_in.rearrange("b t c -> (b t) c").rearrange("(n p) c -> p n c", p=P)
    out_v = out.rearrange("b t c -> (b t) c").rearrange("(n p) c -> p n c", p=P)

    with ExitStack() as ctx:
        def sb(name, shape, dt):
            return ctx.enter_context(nc.sbuf_tensor(name, shape, dt))

        def sem(name):
            return ctx.enter_context(nc.semaphore(name))

        xa = sb("xa", [P, TILES, C], F32)
        xh = sb("xh", [P, CT, N], F16)
        xl = sb("xl", [P, CT, N], F16)
        stage1 = sb("stage1", [P, CT, FC], F32)
        stage2 = sb("stage2", [P, FT, C], F32)
        ident = sb("ident", [P, P], F32)
        ones = sb("ones", [P, P], F32)
        rows = sb("rows", [P, P], F32)
        b1rows = sb("b1rows", [P, P], F32)
        gate_rows = sb("gate_rows", [E, C], F32)
        cols = sb("cols", [P, 2 * CT], F32)
        edec = sb("edec", [P, CT], F32)
        dcol = sb("dcol", [P, CT], F32)
        um = sb("um", [P, CT], F32)
        nup = sb("nup", [P, CT], F32)
        mask = sb("mask", [P, RB * SEG], F32)
        decay = sb("decay", [P, CT, RB * SEG], F32)
        eps = sb("eps", [P, 1], F32)
        b1T = sb("b1T", [P, E, DFF // P], F32)
        gT = sb("gT", [P, CT, E], F32)
        gres = sb("gres", [P, 2, CT, E], F32)
        g3 = sb("g3", [P, CT, 3, E], BF16)
        bn = sb("bn", [P, GB, 6], F32)
        mv = sb("mv", [P, TILES, 2], F32)
        lnv = sb("lnv", [P, TILES], F32)
        rstd = sb("rstd", [P, TILES], F32)
        nmr = sb("nmr", [P, TILES], F32)
        sm = sb("sm", [P, TILES], F32)
        nm = sb("nm", [P, TILES], F32)
        ssq = sb("ssq", [P, TILES], F32)
        lnv2 = sb("lnv2", [P, TILES], F32)
        rs2 = sb("rs2", [P, TILES], F32)
        logits = sb("logits", [P, TILES, E], F32)
        tot = sb("tot", [P, E], F32)
        top = sb("top", [P, 8], F32)
        topi = sb("topi", [P, 8], U32)
        topf = sb("topf", [P, 8], F32)
        iota = sb("iota", [P, E], F32)
        pick = sb("pick", [P, TOPK, E], F32)
        lsel = sb("lsel", [P, TOPK, TILES], F32)
        lmax = sb("lmax", [P, TILES], F32)
        lexp = sb("lexp", [P, TOPK, TILES], F32)
        lsum = sb("lsum", [P, TILES], F32)
        linv = sb("linv", [P, TILES], F32)
        rw = sb("rw", [P, TOPK, TILES], F32)
        ptmp = sb("ptmp", [P, TILES, E], F32)
        b1tmp = sb("b1tmp", [P, DFF // P, E], F32)
        b1c = sb("b1c", [P, TOPK, DFF // P], F32)
        mb = sb("mb", [P, TOPK], F32)
        mb2 = sb("mb2", [P, NCH], F32)
        mx = sb("mx", [P, NCH, 2], F32)
        q = sb("q", [P, NCH, 3], F32)
        eb = sb("eb", [P, 2, 3], I32)
        eh = sb("eh", [P, 2, 3], I32)
        ei = sb("ei", [P, 2, 3], I32)
        scale = sb("scale", [P, 2, 3], F32)
        descale = sb("descale", [P, 2, 3], F32)
        gsc = sb("gsc", [P, 2], F32)
        bias = sb("bias", [P, 2, FT], F32)
        rwc = sb("rwc", [P, NCH, TILES], F32)
        rwd = sb("rwd", [P, 2, TILES], F32)

        TP = CT * RB * SEG
        TU = CT * GT
        arena_y = sb("arena_y", [P, NG * TU], F32)
        arena_v = sb("arena_v", [P, NG * TU], F32)
        arena_t = sb("arena_t", [P, 2 * TU + 2 * TP], F32)
        arena_s = sb("arena_s", [P, 3 * C], F32)
        kn = arena_y[:, :].rearrange("p (g t c) -> p g t c", g=NG, t=GB)
        yT = arena_y[:, :].rearrange("p (g k n) -> p g k n", g=NG, k=CT)
        vn = arena_v[:, :].rearrange("p (n c) -> p n c", c=C)
        ek = arena_t[:, 0:TU].rearrange("p (k n) -> p k n", k=CT)
        ekv = arena_t[:, TU:2 * TU].rearrange("p (k n) -> p k n", k=CT)
        s1 = arena_t[:, 2 * TU:2 * TU + TP].rearrange("p (k n) -> p k n", k=CT)
        sv = arena_t[:, 2 * TU + TP:2 * TU + 2 * TP].rearrange("p (k n) -> p k n", k=CT)
        x2n = arena_s[:, 0:2 * C].rearrange("p (a c) -> p a c", a=2)
        junk = arena_s[:, 2 * C:3 * C]
        yb = arena_y[:, :].bitcast(F16)
        WS = CT * FC
        w1h = yb[:, 0:2 * WS].rearrange("p (a k f) -> p a k f", a=2, k=CT)
        w1l = yb[:, 2 * WS:4 * WS].rearrange("p (a k f) -> p a k f", a=2, k=CT)
        w2h = yb[:, 4 * WS:6 * WS].rearrange("p (a k f) -> p a k f", a=2, k=FT)
        w2l = yb[:, 6 * WS:8 * WS].rearrange("p (a k f) -> p a k f", a=2, k=FT)
        vb = arena_v[:, :].bitcast(F16)
        HS = NB * FT * GT
        hh = vb[:, 0:HS].rearrange("p (n k t) -> p n k t", n=NB, k=FT)
        hl = vb[:, HS:2 * HS].rearrange("p (n k t) -> p n k t", n=NB, k=FT)
        g32 = arena_t[:, 0:FT * GT].rearrange("p (k t) -> p k t", k=FT)
        b2b = arena_t[:, TU:TU + TOPK * C].rearrange("p (k c) -> p k c", k=TOPK)
        bt = arena_t[:, TU + TOPK * C:TU + 2 * TOPK * C].rearrange("p (k c) -> p k c", k=TOPK)

        ps = ctx.enter_context(nc.psum_tensor("ps", [P, 8, 512], F32))
        psK = [ps[:, 0, :], ps[:, 1, :]]
        psV = [ps[:, 2, :], ps[:, 3, :]]
        psY = ps[:, 4, :]
        psX = [ps[:, 5, :], ps[:, 6, :]]
        psM = ps[:, 7, :]
        psA = [ps[:, n, :] for n in range(FT)]
        psB = [ps[:, 4, :], ps[:, 5, :]]
        psS = ps[:, 6, 0:3]

        d_x0 = [sem(f"d_x0_{t}") for t in range(GB)]
        d_x = [sem(f"d_x{g}") for g in range(1, NG)]
        d_v = [sem(f"d_v{g}") for g in range(NG)]
        d_rows = sem("d_rows")
        d_gate = sem("d_gate")
        d_w1 = sem("d_w1")
        d_w2 = sem("d_w2")
        d_b2 = sem("d_b2")
        d_out = sem("d_out")
        c_pool = sem("c_pool")
        c_id = sem("c_id")
        c_cols = sem("c_cols")
        c_rowsT = sem("c_rowsT")
        c_edec = sem("c_edec")
        c_dcol = sem("c_dcol")
        c_dve = sem("c_dve")
        c_gateT = sem("c_gateT")
        c_g3 = sem("c_g3")
        c_ready = sem("c_ready")
        bn_done = sem("bn_done")
        mv_ready = sem("mv_ready")
        lnv_done = sem("lnv_done")
        rstd_ready = sem("rstd_ready")
        nmr_ready = sem("nmr_ready")
        kn_ready = sem("kn_ready")
        kT_ready = sem("kT_ready")
        vT_ready = sem("vT_ready")
        ek_ready = sem("ek_ready")
        keys_ready = sem("keys_ready")
        sv_in = sem("sv_in")
        v_used = sem("v_used")
        sv_ready = sem("sv_ready")
        s1_ready = sem("s1_ready")
        num_done = sem("num_done")
        den_done = sem("den_done")
        lnd_done = sem("lnd_done")
        r_ready = sem("r_ready")
        y_done = sem("y_done")
        yT_ready = sem("yT_ready")
        x1_ready = sem("x1_ready")
        nm_ready = sem("nm_ready")
        sq_done = sem("sq_done")
        lnv2_done = sem("lnv2_done")
        rs2_ready = sem("rs2_ready")
        x2n_ready = sem("x2n_ready")
        x2T_ready = sem("x2T_ready")
        xh_ready = sem("xh_ready")
        xl_ready = sem("xl_ready")
        lg_mm = sem("lg_mm")
        lg_done = sem("lg_done")
        tot_mm = sem("tot_mm")
        rt = sem("rt")
        top_ready = sem("top_ready")
        l_ready = sem("l_ready")
        lexp_ready = sem("lexp_ready")
        rw_ready = sem("rw_ready")
        rwd_ready = sem("rwd_ready")
        mx_done = sem("mx_done")
        q_ready = sem("q_ready")
        sum_ready = sem("sum_ready")
        sc_step = sem("sc_step")
        sc_ready = sem("sc_ready")
        w1h_ready = sem("w1h_ready")
        w1l_ready = sem("w1l_ready")
        w2h_ready = sem("w2h_ready")
        w2l_ready = sem("w2l_ready")
        up_mm = sem("up_mm")
        g_ready = sem("g_ready")
        hh_ready = sem("hh_ready")
        hl_ready = sem("hl_ready")
        down_mm = sem("down_mm")
        b2_step = sem("b2_step")
        b2_done = sem("b2_done")
        acc_done = sem("acc_done")

        block = ctx.enter_context(nc.Block())

        STEPS = TILES + LAG_LOGIT

        def at(s, lag):
            return s - lag if 0 <= s - lag < TILES else None

        pe_engine = nc.tensor

        def walk_chunks(eng, up, down, early, prepare):
            def pair(c, last):
                for par in range(2):
                    more = not (last and par == 1)
                    if more:
                        early(c + par + 1, 1 - par)
                    up(c + par, par, 1)
                    down(c + par, par, 0)
                    if more:
                        prepare(c + par + 1, 1 - par)
                    if eng is pe_engine:
                        with eng.Fori(1, NB - 1) as n:
                            up(c + par, par, n + 1)
                            down(c + par, par, n)
                    else:
                        for n in range(1, NB - 1):
                            up(c + par, par, n + 1)
                            down(c + par, par, n)
                    if more:
                        up(c + par + 1, 1 - par, 0)
                    down(c + par, par, NB - 1)

            early(0, 0)
            prepare(0, 0)
            up(0, 0, 0)
            with eng.Fori(0, NCH // 2 - 1) as i:
                pair(2 * i, False)
            pair(NCH - 2, True)

        @block.sync
        def _(sp):
            for t in range(GB):
                sp.dma_start(xa[:, t, :], x_v[:, t, :]).then_inc(d_x0[t], 16)
            for g in range(NG):
                if g >= 1:
                    sp.dma_start(xa[:, g * GB:(g + 1) * GB, :], x_v[:, g * GB:(g + 1) * GB, :]).then_inc(d_x[g - 1], 16)
                sp.dma_start(vn[:, g * GB:(g + 1) * GB, :], v_v[:, g * GB:(g + 1) * GB, :]).then_inc(d_v[g], 16)

            sp.wait_ge(top_ready, 1)
            picked = [sp.value_load(topi[0:1, k:k + 1], min_val=0, max_val=E - 1) for k in range(TOPK)]

            def load_chunk(k, j, c):
                wait(sp, w1h_ready, c)
                wait(sp, w1l_ready, c)
                sp.dma_start(stage1[:, :, :],
                             w1[bass.ds(picked[k], 1), :, bass.ds(j * FC, FC)]
                             .rearrange("e (k p) f -> p (e k) f", p=P)).then_inc(d_w1, 16)
                wait(sp, w2h_ready, c)
                wait(sp, w2l_ready, c)
                sp.dma_start(stage2[:, :, :],
                             w2[bass.ds(picked[k], 1), bass.ds(j * FC, FC), :]
                             .rearrange("e (k p) d -> p (e k) d", p=P)).then_inc(d_w2, 16)

            load_chunk(0, 0, 0)
            for k in range(TOPK):
                sp.dma_start(b2b[:, k, :], b2[bass.ds(picked[k], 1), :].broadcast_to([P, C])).then_inc(d_b2, 16)
            with sp.Fori(1, CPE) as j:
                load_chunk(0, j, j)
            with sp.Fori(0, CPE) as j:
                load_chunk(1, j, j + CPE)
            with sp.Fori(0, TILES) as t:
                sp.wait_ge(acc_done, t + NCH * TILES + 1)
                sp.dma_start(out_v[:, bass.ds(t, 1), :], xa[:, bass.ds(t, 1), :]).then_inc(d_out, 16)
            sp.wait_ge(d_out, 16 * TILES)

        @block.gpsimd
        def _(pool):
            nc.gpsimd.memset(ident[:, :], 0.0).then_inc(c_pool, 1)
            pool.wait_ge(c_pool, 1)
            nc.gpsimd.affine_select(out=ident[:, :], in_=ident[:, :], compare_op=ALU.not_equal, fill=1.0,
                                    base=0, pattern=[[-1, P]], channel_multiplier=1).then_inc(c_id, 1)
            nc.gpsimd.memset(ones[:, :], 1.0).then_inc(c_pool, 1)
            nc.gpsimd.memset(eps[:, :], LN_EPS).then_inc(c_pool, 1)
            nc.gpsimd.memset(mask[:, :], 1.0).then_inc(c_pool, 1)
            pool.wait_ge(c_pool, 4)
            nc.gpsimd.memset(mask[:, :].rearrange("p (b n) -> p b n", n=SEG)[:, :, 0:2], 0.0).then_inc(c_pool, 1)
            nc.gpsimd.memset(s1.rearrange("p k (b n) -> p (k b) n", n=SEG)[:, :, 0:1], 1.0).then_inc(c_pool, 1)
            for e in range(E):
                nc.gpsimd.memset(iota[:, e:e + 1], float(e)).then_inc(c_pool, 1)

            def shifted(buf, j):
                return buf[:, j, :].rearrange("p (b n) -> p b n", n=SEG)[:, :, 0:T]

            def sums(u):
                j = u % CT
                pool.wait_ge(sv_ready, u + 1)
                num = ekv[:, j, :].rearrange("p (b n) -> p b n", n=T)
                nc.gpsimd.tensor_tensor(num, num, shifted(sv, j), ALU.add).then_inc(num_done, 1)
                pool.wait_ge(s1_ready, u + 1)
                den = ek[:, j, :].rearrange("p (b n) -> p b n", n=T)
                nc.gpsimd.tensor_tensor(den, den, shifted(s1, j), ALU.add).then_inc(den_done, 1)

            def ratio(u):
                g, j = divmod(u, CT)
                pool.wait_ge(r_ready, u + 1)
                pool.wait_ge(num_done, u + 1)
                if j == 0:
                    pool.wait_ge(kT_ready, g * CT + CT)
                nc.gpsimd.tensor_tensor(yT[:, g, j, :], ekv[:, j, :], ek[:, j, :], ALU.mult).then_inc(y_done, 1)

            def second_norm(t):
                pool.wait_ge(rs2_ready, t + 1)
                wait(pool, x2T_ready, t - 1)
                nc.gpsimd.tensor_scalar(x2n[:, t % 2, :], xa[:, t, :], nm[:, t:t + 1], rs2[:, t:t + 1],
                                        ALU.add, ALU.mult).then_inc(x2n_ready, 1)

            for s in range(STEPS):
                if at(s, LAG_RATIO) is not None:
                    ratio(at(s, LAG_RATIO))
                if at(s, LAG_NORM) is not None:
                    second_norm(at(s, LAG_NORM))
                if at(s, LAG_STATES) is not None:
                    sums(at(s, LAG_STATES))

            pool.wait_ge(rw_ready, 1)
            pool.wait_ge(d_b2, 16 * TOPK)
            with pool.Fori(0, TILES) as t:
                for k in range(TOPK):
                    nc.gpsimd.tensor_tensor(bt[:, k, :], b2b[:, k, :], rw[:, k, bass.ds(t, 1)].broadcast_to([P, C]),
                                            ALU.mult).then_inc(b2_step, 1)
                pool.wait_ge(b2_step, t * 3 + 2)
                nc.gpsimd.tensor_tensor(bt[:, 0, :], bt[:, 0, :], bt[:, 1, :], ALU.add).then_inc(b2_step, 1)
                pool.wait_ge(b2_step, t * 3 + 3)
                xt = xa[:, bass.ds(t, 1), :].rearrange("p a c -> p (a c)")
                nc.gpsimd.tensor_tensor(xt, xt, bt[:, 0, :], ALU.add).then_inc(b2_done, 1)
                pool.wait_ge(b2_done, t + 1)

        @block.scalar
        def _(act):
            nc.scalar.preload_act_table_set("natural_log_exp_and_others")
            act.dma_start(rows[0:CT, :], time_decay.rearrange("(k p) -> k p", p=P)).then_inc(d_rows, 16)
            act.dma_start(rows[CT:2 * CT, :], time_first.rearrange("(k p) -> k p", p=P)).then_inc(d_rows, 16)
            act.dma_start(gate_rows[:, :], gate_w).then_inc(d_gate, 16)
            act.dma_start(b1rows[:, :], b1.rearrange("e (k p) -> (e k) p", p=P)).then_inc(d_gate, 16)
            act.wait_ge(c_pool, 6 + E)

            def first_rstd(g):
                act.wait_ge(mv_ready, g * GB + GB)
                nc.scalar.activation(lnv[:, g * GB:(g + 1) * GB], mv[:, g * GB:(g + 1) * GB, 1],
                                     ACT.Ln, bias=eps[:, 0:1]).then_inc(lnv_done, 1)
                act.wait_ge(lnv_done, g + 1)
                nc.scalar.activation(rstd[:, g * GB:(g + 1) * GB], lnv[:, g * GB:(g + 1) * GB],
                                     ACT.Exp, scale=-0.5).then_inc(rstd_ready, 1)

            def first_norm(t):
                g, j = divmod(t, GB)
                act.wait_ge(nmr_ready, g + 1)
                nc.scalar.activation(kn[:, g, j, :], xa[:, t, :], ACT.Identity,
                                     scale=rstd[:, t:t + 1], bias=nmr[:, t:t + 1]).then_inc(kn_ready, 1)

            def keys(u):
                j = u % CT
                act.wait_ge(kT_ready, u + 1)
                wait(act, y_done, u - CT + 1)
                nc.scalar.activation(ek[:, j, :], psK[j % 2], ACT.Exp, bias=um[:, j:j + 1]).then_inc(ek_ready, 1)
                nc.scalar.activation(s1[:, j, :].rearrange("p (b n) -> p b n", n=SEG)[:, :, 1:SEG],
                                     psK[j % 2].rearrange("p (b n) -> p b n", n=T), ACT.Exp,
                                     bias=nup[:, j:j + 1]).then_inc(keys_ready, 1)

            def variance_and_inverse(t, u):
                if t is not None:
                    act.wait_ge(nm_ready, t + 1)
                    wait(act, sq_done, t)
                    nc.scalar.activation(junk, xa[:, t, :], ACT.Square,
                                         bias=nm[:, t:t + 1], accum_out=ssq[:, t:t + 1]).then_inc(sq_done, 1)
                if u is not None:
                    den = ek[:, u % CT, :]
                    act.wait_ge(den_done, u + 1)
                    nc.scalar.activation(den, den, ACT.Ln).then_inc(lnd_done, 1)
                if t is not None:
                    act.wait_ge(sq_done, t + 1)
                    nc.scalar.activation(lnv2[:, t:t + 1], ssq[:, t:t + 1], ACT.Ln,
                                         bias=eps[:, 0:1], scale=1.0 / C).then_inc(lnv2_done, 1)
                if u is not None:
                    act.wait_ge(lnd_done, u + 1)
                    nc.scalar.activation(den, den, ACT.Exp, scale=-1.0).then_inc(r_ready, 1)
                if t is not None:
                    act.wait_ge(lnv2_done, t + 1)
                    nc.scalar.activation(rs2[:, t:t + 1], lnv2[:, t:t + 1], ACT.Exp,
                                         scale=-0.5).then_inc(rs2_ready, 1)

            def high(t):
                act.wait_ge(x2T_ready, t + 1)
                nc.scalar.activation(xh[:, :, t * P:(t + 1) * P], psX[t % 2].rearrange("p (k n) -> p k n", k=CT),
                                     ACT.Copy, scale=X_SCALE).then_inc(xh_ready, 1)

            first_rstd(0)
            for t in range(GB):
                first_norm(t)
            act.wait_ge(c_cols, 1)
            nc.scalar.activation(edec[:, :], cols[:, 0:CT], ACT.Exp).then_inc(c_edec, 1)
            act.wait_ge(c_edec, 1)
            nc.scalar.activation(dcol[:, :], edec[:, :], ACT.Exp, scale=-1.0).then_inc(c_dcol, 1)
            act.wait_ge(c_dve, 2)
            for s in range(STEPS):
                if at(s, 0) is not None:
                    keys(at(s, 0))
                if at(s, LAG_SPLIT) is not None:
                    high(at(s, LAG_SPLIT))
                variance_and_inverse(at(s, LAG_RESIDUAL), at(s, LAG_INVERSE))
                g, j = s // GB + 1, s % GB
                if g < NG:
                    if j == 0:
                        first_rstd(g)
                    if j == 1 or j == 2:
                        first_norm(g * GB + 2 * (j - 1))
                        first_norm(g * GB + 2 * (j - 1) + 1)

            act.wait_ge(l_ready, 1)
            nc.scalar.activation(lexp[:, :, :], lsel[:, :, :], ACT.Exp, scale=1.0 / X_SCALE).then_inc(lexp_ready, 1)
            nc.scalar.preload_act_table(ACT.Gelu_apprx_tanh)

            def early(c, par):
                pass

            def prepare(c, par):
                act.wait_ge(sc_ready, c + 1)
                wait(act, up_mm, (c - 1) * NB * FT)
                nc.scalar.activation(w1h[:, par, :, :], stage1[:, :, :], ACT.Identity,
                                     scale=scale[:, par, 0:1]).then_inc(w1h_ready, 1)
                wait(act, down_mm, c * TILES)
                nc.scalar.activation(w2h[:, par, :, :], stage2[:, :, :], ACT.Identity,
                                     scale=scale[:, par, 1:2]).then_inc(w2h_ready, 1)

            def up(c, par, n):
                for f in range(FT):
                    u = c * (NB * FT) + n * FT + f
                    act.wait_ge(up_mm, u + 1)
                    wait(act, hl_ready, u - FT + 1)
                    nc.scalar.activation(g32[:, f, :], psA[f], ACT.Gelu_apprx_tanh,
                                         scale=gsc[:, par:par + 1],
                                         bias=bias[:, par, f:f + 1]).then_inc(g_ready, 1)
                    act.wait_ge(g_ready, u + 1)
                    act.wait_ge(down_mm, c * TILES + n * GB + GB)
                    nc.scalar.activation(hh[:, bass.ds(n, 1), f, :].rearrange("p a t -> p (a t)"), g32[:, f, :],
                                         ACT.Identity, scale=scale[:, par, 2:3]).then_inc(hh_ready, 1)

            walk_chunks(act, up, lambda c, par, n: None, early, prepare)

        @block.vector
        def _(dve):
            def statistics(t):
                j = t % GB
                wait(dve, mv_ready, t - GB + 1)
                nc.vector.bn_stats(bn[:, j, :], xa[:, t, :]).then_inc(bn_done, 1)

            def aggregate(t):
                dve.wait_ge(bn_done, t + 1)
                nc.vector.bn_aggr(mv[:, t, :], bn[:, t % GB, :]).then_inc(mv_ready, 1)

            def minus_mean(g):
                dve.wait_ge(rstd_ready, g + 1)
                nc.vector.scalar_tensor_tensor(nmr[:, g * GB:(g + 1) * GB], mv[:, g * GB:(g + 1) * GB, 0], -1.0,
                                               rstd[:, g * GB:(g + 1) * GB], ALU.mult, ALU.mult).then_inc(nmr_ready, 1)

            def states(u):
                j = u % CT
                dve.wait_ge(keys_ready, u + 1)
                dve.wait_ge(vT_ready, u + 1)
                vt = psV[j % 2].rearrange("p (b n) -> p b n", n=T)
                sv3 = sv[:, j, :].rearrange("p (b n) -> p b n", n=SEG)
                s13 = s1[:, j, :].rearrange("p (b n) -> p b n", n=SEG)
                nc.vector.tensor_copy(sv3[:, :, 0], vt[:, :, 0]).then_inc(sv_in, 1)
                nc.vector.tensor_tensor(sv3[:, :, 1:SEG], s13[:, :, 1:SEG], vt, ALU.mult).then_inc(sv_in, 1)
                nc.vector.tensor_tensor(ekv[:, j, :], ek[:, j, :], psV[j % 2], ALU.mult).then_inc(v_used, 1)
                dve.wait_ge(sv_in, 2 * u + 2)
                nc.vector.tensor_tensor_scan(sv[:, j, :], decay[:, j, :], sv[:, j, :], 0.0,
                                             ALU.mult, ALU.add).then_inc(sv_ready, 1)
                nc.vector.tensor_tensor_scan(s1[:, j, :], decay[:, j, :], s1[:, j, :], 0.0,
                                             ALU.mult, ALU.add).then_inc(s1_ready, 1)

            def residual(t):
                dve.wait_ge(yT_ready, t + 1)
                nc.vector.scalar_tensor_tensor(xa[:, t, :], psY, 1.0, xa[:, t, :], ALU.mult, ALU.add,
                                               accum_out=sm[:, t:t + 1]).then_inc(x1_ready, 1)
                dve.wait_ge(x1_ready, t + 1)
                nc.vector.tensor_scalar(nm[:, t:t + 1], sm[:, t:t + 1], -1.0 / C, None, ALU.mult).then_inc(nm_ready, 1)

            def low(t):
                dve.wait_ge(xh_ready, t + 1)
                nc.vector.scalar_tensor_tensor(xl[:, :, t * P:(t + 1) * P],
                                               psX[t % 2].rearrange("p (k n) -> p k n", k=CT), X_SCALE,
                                               xh[:, :, t * P:(t + 1) * P], ALU.mult, ALU.subtract).then_inc(xl_ready, 1)

            def logit(t):
                dve.wait_ge(lg_mm, t + 1)
                nc.vector.tensor_reduce(logits[:, t, :], psM[:, 0:3 * E].rearrange("p (s e) -> p e s", s=3), AX_X,
                                        ALU.add).then_inc(lg_done, 1)

            for t in range(GB):
                dve.wait_ge(d_x0[t], 16)
                statistics(t)
            for t in range(GB):
                aggregate(t)
            dve.wait_ge(c_rowsT, 1)
            nc.vector.tensor_copy(cols[:, :], psM[:, 0:2 * CT]).then_inc(c_cols, 1)
            minus_mean(0)
            dve.wait_ge(c_cols, 1)
            nc.vector.tensor_scalar(um[:, :], cols[:, CT:2 * CT], 0.0, None, ALU.min).then_inc(c_dve, 1)
            nc.vector.tensor_scalar(nup[:, :], cols[:, CT:2 * CT], 0.0, -1.0, ALU.max, ALU.mult).then_inc(c_dve, 1)
            dve.wait_ge(c_pool, 6 + E)
            dve.wait_ge(c_dcol, 1)
            for j in range(CT):
                nc.vector.tensor_scalar(decay[:, j, :], mask[:, :], dcol[:, j:j + 1], None, ALU.mult).then_inc(c_dve, 1)
            dve.wait_ge(c_dve, 2 + CT)

            def gate_parts():
                dve.wait_ge(c_gateT, 1)
                nc.vector.tensor_copy(gT[:, :, :], psM[:, 64:64 + CT * E].rearrange("p (k e) -> p k e", k=CT)).then_inc(c_g3, 1)
                nc.vector.tensor_copy(b1T[:, :, :].rearrange("p e f -> p (e f)"), psM[:, 128:256]).then_inc(c_ready, 1)
                dve.wait_ge(c_g3, 1)
                nc.vector.tensor_copy(g3[:, :, 0, :], gT[:, :, :]).then_inc(c_g3, 1)
                dve.wait_ge(c_g3, 2)
                nc.vector.tensor_tensor(gres[:, 0, :, :], gT[:, :, :], g3[:, :, 0, :], ALU.subtract).then_inc(c_g3, 1)
                dve.wait_ge(c_g3, 3)
                nc.vector.tensor_copy(g3[:, :, 1, :], gres[:, 0, :, :]).then_inc(c_g3, 1)
                dve.wait_ge(c_g3, 4)
                nc.vector.tensor_tensor(gres[:, 1, :, :], gres[:, 0, :, :], g3[:, :, 1, :], ALU.subtract).then_inc(c_g3, 1)
                dve.wait_ge(c_g3, 5)
                nc.vector.tensor_copy(g3[:, :, 2, :], gres[:, 1, :, :]).then_inc(c_g3, 1)

            for s in range(STEPS):
                if s % GB == 1 and s // GB + 1 < NG:
                    minus_mean(s // GB + 1)
                if at(s, LAG_RESIDUAL) is not None:
                    residual(at(s, LAG_RESIDUAL))
                if at(s, LAG_STATES) is not None:
                    states(at(s, LAG_STATES))
                if at(s, LAG_SPLIT) is not None:
                    low(at(s, LAG_SPLIT))
                if s == 0:
                    dve.wait_ge(d_x[0], 16)
                    for t in range(GB, 2 * GB):
                        statistics(t)
                    for t in range(GB, 2 * GB):
                        aggregate(t)
                    gate_parts()
                if at(s, LAG_LOGIT) is not None:
                    logit(at(s, LAG_LOGIT))
                t = s + 2 * GB - 1
                if s >= 1 and t < TILES:
                    dve.wait_ge(d_x[t // GB - 1], 16)
                    statistics(t)
                    aggregate(t)

            step = [0]

            def link(ins):
                step[0] += 1
                ins.then_inc(rt, 1)
                dve.wait_ge(rt, step[0])

            dve.wait_ge(tot_mm, 1)
            link(nc.vector.tensor_reduce(tot[:, :], psM[:, 128:128 + TILES * E].rearrange("p (t e) -> p e t", e=E),
                                         AX_X, ALU.add))
            link(nc.vector.max(top[:, :], tot[:, :]))
            nc.vector.max_index(topi[:, :], top[:, :], tot[:, :]).then_inc(top_ready, 1)
            dve.wait_ge(top_ready, 1)
            link(nc.vector.tensor_copy(topf[:, :], topi[:, :]))
            for k in range(TOPK):
                link(nc.vector.tensor_scalar(pick[:, k, :], iota[:, :], topf[:, k:k + 1], None, ALU.is_equal))
            for k in range(TOPK):
                link(nc.vector.tensor_tensor(b1tmp[:, :, :], b1T[:, :, :].rearrange("p e f -> p f e"),
                                             pick[:, k:k + 1, :].broadcast_to([P, DFF // P, E]), ALU.mult))
                link(nc.vector.tensor_reduce(b1c[:, k, :], b1tmp[:, :, :], AX_X, ALU.add))
                link(nc.vector.tensor_reduce(mb[:, k:k + 1], b1c[:, k, :], AX_X, ALU.max, apply_absolute_value=True))
                link(nc.vector.tensor_tensor(mb[:, k:k + 1], mb[:, k:k + 1], mb[:, k:k + 1], ALU.mult))
                link(nc.vector.tensor_scalar(mb2[:, k * CPE:(k + 1) * CPE], mb[:, k:k + 1].broadcast_to([P, CPE]),
                                             2.0, None, ALU.mult))

            def router_weights():
                for k in range(TOPK):
                    link(nc.vector.tensor_tensor(ptmp[:, :, :], logits[:, :, :],
                                                 pick[:, k:k + 1, :].broadcast_to([P, TILES, E]), ALU.mult))
                    link(nc.vector.tensor_reduce(lsel[:, k, :], ptmp[:, :, :], AX_X, ALU.add))
                link(nc.vector.tensor_tensor(lmax[:, :], lsel[:, 0, :], lsel[:, 1, :], ALU.max))
                link(nc.vector.tensor_tensor(lsel[:, 0, :], lsel[:, 0, :], lmax[:, :], ALU.subtract))
                nc.vector.tensor_tensor(lsel[:, 1, :], lsel[:, 1, :], lmax[:, :], ALU.subtract).then_inc(l_ready, 1)
                dve.wait_ge(lexp_ready, 1)
                link(nc.vector.tensor_tensor(lsum[:, :], lexp[:, 0, :], lexp[:, 1, :], ALU.add))
                link(nc.vector.reciprocal(linv[:, :], lsum[:, :]))
                link(nc.vector.tensor_tensor(rw[:, 0, :], lexp[:, 0, :], linv[:, :], ALU.mult))
                nc.vector.tensor_tensor(rw[:, 1, :], lexp[:, 1, :], linv[:, :], ALU.mult).then_inc(rw_ready, 1)
                dve.wait_ge(rw_ready, 1)
                for k in range(TOPK):
                    for c in range(k * CPE, (k + 1) * CPE):
                        nc.vector.tensor_copy(rwc[:, c, :], rw[:, k, :]).then_inc(rt, 1)
                        step[0] += 1
                dve.wait_ge(rt, step[0])

            def early(c, par):
                dve.wait_ge(d_w1, c * 16 + 16)
                nc.vector.tensor_reduce(mx[:, bass.ds(c, 1), 0], stage1[:, :, :], AX_XY, ALU.max,
                                        apply_absolute_value=True).then_inc(mx_done, 1)
                dve.wait_ge(d_w2, c * 16 + 16)
                nc.vector.tensor_reduce(mx[:, bass.ds(c, 1), 1], stage2[:, :, :], AX_XY, ALU.max,
                                        apply_absolute_value=True).then_inc(mx_done, 1)
                dve.wait_ge(mx_done, c * 3 + 2)
                mc = mx[:, bass.ds(c, 1), :].rearrange("p a c -> p (a c)")
                nc.vector.tensor_tensor(q[:, bass.ds(c, 1), 0:2].rearrange("p a c -> p (a c)"), mc, mc,
                                        ALU.mult).then_inc(mx_done, 1)
                dve.wait_ge(mx_done, c * 3 + 3)
                nc.vector.scalar_tensor_tensor(q[:, bass.ds(c, 1), 2], q[:, bass.ds(c, 1), 0], 2.0 * C * CT,
                                               mb2[:, bass.ds(c, 1)], ALU.mult, ALU.add).then_inc(q_ready, 1)

            def prepare(c, par):
                def row(buf):
                    return buf[:, par, :]

                def small(k, ins):
                    ins.then_inc(sc_step, 1)
                    dve.wait_ge(sc_step, c * SMALL + k)

                SMALL = 8
                dve.wait_ge(sum_ready, c + 1)
                wait(dve, g_ready, c * NB * FT - NB * FT)
                wait(dve, hl_ready, c * NB * FT - NB * FT)
                nc.vector.tensor_copy(bias[:, par, :], b1c[:, :, :].rearrange("p k f -> p (k f)")
                                      [:, bass.ds(c * FT, FT)]).then_inc(sc_step, 1)
                small(2, nc.vector.tensor_scalar(row(eb), psS.bitcast(I32), 23, None, ALU.logical_shift_right))
                small(3, nc.vector.tensor_scalar(row(eh), row(eb), 129.0, None, ALU.add))
                small(4, nc.vector.tensor_scalar(row(eb), row(eh), 1, None, ALU.logical_shift_right))
                small(5, nc.vector.tensor_scalar(row(ei), row(eb), -1.0, 268.0, ALU.mult, ALU.add))
                small(6, nc.vector.tensor_scalar(row(scale).bitcast(I32), row(ei), 23, None, ALU.logical_shift_left))
                small(7, nc.vector.tensor_scalar(row(eh), row(eb), -14.0, None, ALU.add))
                small(8, nc.vector.tensor_scalar(row(descale).bitcast(I32), row(eh), 23, None, ALU.logical_shift_left))
                nc.vector.tensor_scalar(gsc[:, par:par + 1], descale[:, par, 0:1], 1.0 / X_SCALE, None,
                                        ALU.mult).then_inc(sc_ready, 1)
                dve.wait_ge(w1h_ready, c + 1)
                nc.vector.scalar_tensor_tensor(w1l[:, par, :, :], stage1[:, :, :], scale[:, par, 0:1],
                                               w1h[:, par, :, :], ALU.mult, ALU.subtract).then_inc(w1l_ready, 1)
                dve.wait_ge(w2h_ready, c + 1)
                nc.vector.scalar_tensor_tensor(w2l[:, par, :, :], stage2[:, :, :], scale[:, par, 1:2],
                                               w2h[:, par, :, :], ALU.mult, ALU.subtract).then_inc(w2l_ready, 1)

            def up(c, par, n):
                for f in range(FT):
                    dve.wait_ge(hh_ready, c * (NB * FT) + n * FT + f + 1)
                    nc.vector.scalar_tensor_tensor(hl[:, bass.ds(n, 1), f, :].rearrange("p a t -> p (a t)"),
                                                   g32[:, f, :], scale[:, par, 2:3],
                                                   hh[:, bass.ds(n, 1), f, :].rearrange("p a t -> p (a t)"),
                                                   ALU.mult, ALU.subtract).then_inc(hl_ready, 1)

            def down(c, par, n):
                if n == 0:
                    nc.vector.tensor_scalar(rwd[:, par, :], rwc[:, bass.ds(c, 1), :].rearrange("p a c -> p (a c)"),
                                            descale[:, par, 1:2], descale[:, par, 2:3], ALU.mult, ALU.mult).then_inc(rwd_ready, 1)
                    dve.wait_ge(rwd_ready, c + 1)
                for t in range(GB):
                    tile = n * GB + t
                    dve.wait_ge(down_mm, (c + 1) * TILES + tile + 1)
                    dve.wait_ge(b2_done, tile + 1)
                    dve.wait_ge(acc_done, c * TILES + tile + 1)
                    xt = xa[:, bass.ds(tile, 1), :].rearrange("p a c -> p (a c)")
                    nc.vector.scalar_tensor_tensor(xt, psB[t % 2],
                                                   rwd[:, par, tile:tile + 1],
                                                   xt, ALU.mult, ALU.add).then_inc(acc_done, 1)

            router_weights()
            dve.sem_inc(acc_done, TILES)
            walk_chunks(dve, up, down, early, prepare)

        @block.tensor
        def _(pe):
            pe.wait_ge(c_id, 1)
            pe.wait_ge(d_rows, 32)
            nc.tensor.transpose(psM[:, 0:2 * CT], rows[0:2 * CT, :], ident[0:2 * CT, 0:2 * CT]).then_inc(c_rowsT, 1)

            def turn_constants():
                pe.wait_ge(d_gate, 32)
                pe.wait_ge(c_cols, 1)
                for k in range(CT):
                    nc.tensor.transpose(psM[:, 64 + k * E:64 + (k + 1) * E], gate_rows[:, k * P:(k + 1) * P],
                                        ident[0:E, 0:E])
                nc.tensor.transpose(psM[:, 128:256], b1rows[:, :], ident[:, :]).then_inc(c_gateT, 1)

            def turn_k(u):
                g, j = divmod(u, CT)
                if j == 0:
                    pe.wait_ge(kn_ready, g * GB + GB)
                wait(pe, keys_ready, u - 1)
                for t in range(GB):
                    last = nc.tensor.transpose(psK[j % 2][:, t * P:(t + 1) * P], kn[:, g, t, j * P:(j + 1) * P],
                                               ident[:, :])
                last.then_inc(kT_ready, 1)

            def turn_v(u):
                g, j = divmod(u, CT)
                if j == 0:
                    pe.wait_ge(d_v[g], 16)
                wait(pe, v_used, u - 1)
                for t in range(GB):
                    last = nc.tensor.transpose(psV[j % 2][:, t * P:(t + 1) * P], vn[:, g * GB + t, j * P:(j + 1) * P],
                                               ident[:, :])
                last.then_inc(vT_ready, 1)

            def turn_y(t):
                g, j = divmod(t, GB)
                if j == 0:
                    pe.wait_ge(y_done, g * CT + CT)
                wait(pe, x1_ready, t)
                for k in range(CT):
                    last = nc.tensor.transpose(psY[:, k * P:(k + 1) * P], yT[:, g, k, j * P:(j + 1) * P], ident[:, :])
                last.then_inc(yT_ready, 1)

            def turn_x(t):
                pe.wait_ge(x2n_ready, t + 1)
                wait(pe, xl_ready, t - 1)
                for k in range(CT):
                    last = nc.tensor.transpose(psX[t % 2][:, k * P:(k + 1) * P], x2n[:, t % 2, k * P:(k + 1) * P],
                                               ident[:, :])
                last.then_inc(x2T_ready, 1)

            def router(t):
                pe.wait_ge(xl_ready, t + 1)
                wait(pe, lg_done, t)
                for n, part in enumerate((xh, xl)):
                    for k in range(CT):
                        last = nc.tensor.matmul(psM[:, 0:3 * E], part[:, k, t * P:(t + 1) * P],
                                                g3[:, k, :, :].rearrange("p s e -> p (s e)"),
                                                start=(n == 0 and k == 0), stop=(n == 1 and k == CT - 1))
                last.then_inc(lg_mm, 1)

            turn_k(0)
            turn_constants()
            for s in range(STEPS):
                if at(s + 1, 0) is not None:
                    turn_k(at(s + 1, 0))
                if s == LAG_LOGIT:
                    pe.wait_ge(c_g3, 6)
                    pe.wait_ge(c_ready, 1)
                if at(s, LAG_LOGIT) is not None:
                    router(at(s, LAG_LOGIT))
                if at(s, LAG_NORM) is not None:
                    turn_x(at(s, LAG_NORM))
                if at(s, 0) is not None:
                    turn_v(at(s, 0))
                if at(s, LAG_TURN_Y) is not None:
                    turn_y(at(s, LAG_TURN_Y))

            pe.wait_ge(lg_done, TILES)
            nc.tensor.matmul(psM[:, 128:128 + TILES * E], ones[:, :], logits[:, :, :].rearrange("p t e -> p (t e)"),
                             start=True, stop=True).then_inc(tot_mm, 1)

            def early(c, par):
                pass

            def prepare(c, par):
                pe.wait_ge(q_ready, c + 1)
                nc.tensor.matmul(psS, ones[:, :], q[:, bass.ds(c, 1), :].rearrange("p a c -> p (a c)"),
                                 start=True, stop=True).then_inc(sum_ready, 1)

            def up(c, par, n):
                if isinstance(n, int) and n == 0:
                    pe.wait_ge(w1l_ready, c + 1)
                def tokens(part, k):
                    return part[:, k, bass.ds(n * GT, GT)]
                for f in range(FT):
                    wait(pe, g_ready, c * (NB * FT) + n * FT + f - FT + 1)
                    for k in range(CT):
                        a_h = w1h[:, par, k, f * P:(f + 1) * P]
                        a_l = w1l[:, par, k, f * P:(f + 1) * P]
                        nc.tensor.matmul(psA[f], a_h, tokens(xh, k), start=(k == 0), stop=False)
                        nc.tensor.matmul(psA[f], a_h, tokens(xl, k), start=False, stop=False)
                        last = nc.tensor.matmul(psA[f], a_l, tokens(xh, k), start=False, stop=(k == CT - 1))
                    last.then_inc(up_mm, 1)

            def down(c, par, n):
                if isinstance(n, int) and n == 0:
                    pe.wait_ge(w2l_ready, c + 1)
                pe.wait_ge(hl_ready, c * (NB * FT) + n * FT + FT)
                for t in range(GB):
                    pe.wait_ge(acc_done, (c + 1) * TILES + n * GB + t - 1)
                    for f in range(FT):
                        hid_h = hh[:, bass.ds(n, 1), f, t * P:(t + 1) * P].rearrange("p a t -> p (a t)")
                        hid_l = hl[:, bass.ds(n, 1), f, t * P:(t + 1) * P].rearrange("p a t -> p (a t)")
                        nc.tensor.matmul(psB[t % 2], hid_h, w2h[:, par, f, :], start=(f == 0), stop=False)
                        nc.tensor.matmul(psB[t % 2], hid_h, w2l[:, par, f, :], start=False, stop=False)
                        last = nc.tensor.matmul(psB[t % 2], hid_l, w2h[:, par, f, :], start=False, stop=(f == FT - 1))
                    last.then_inc(down_mm, 1)

            pe.sem_inc(down_mm, TILES)
            walk_chunks(pe, up, down, early, prepare)


_INS = ['x', 'ctx_2048', 'L0_xattn_time_decay', 'L0_xattn_time_first', 'L0_ffn_gate_w', 'L0_ffn_w1', 'L0_ffn_b1',
        'L0_ffn_w2', 'L0_ffn_b2']
_OUTS = [((8, 256, 512), 'float32')]


def kernel(**inputs):
    import numpy as _np
    import concourse.bacc as _bacc
    from concourse import mybir as _mybir
    from concourse.bass_utils import run_bass_kernel_spmd as _run

    nc = _bacc.Bacc("TRN2", target_bir_lowering=False, num_devices=1)
    arrays, args = {}, []
    for name in _INS:
        a = _np.ascontiguousarray(inputs[name])
        arrays[f"in_{name}_dram"] = a
        args.append(nc.dram_tensor(f"in_{name}_dram", a.shape, _mybir.dt.from_np(a.dtype), kind="ExternalInput").ap())
    for i, (shape, dtype) in enumerate(_OUTS):
        dt = _mybir.dt.from_np(_np.dtype(dtype))
        args.append(nc.dram_tensor(f"out_{i}_dram", shape, dt, kind="ExternalOutput").ap())
    wkv_moe_kernel(nc, *args)
    r = _run(nc, [arrays], core_ids=[0])
    return r.results[0]["out_0_dram"]
```

```python
from contextlib import ExitStack

import concourse.bass as bass
from concourse import mybir

P = 128
F32 = mybir.dt.float32
F16 = mybir.dt.float16
BF16 = mybir.dt.bfloat16
I32 = mybir.dt.int32
U32 = mybir.dt.uint32
ALU = mybir.AluOpType
ACT = mybir.ActivationFunctionType
AX_X = mybir.AxisListType.X
AX_XY = mybir.AxisListType.XY

LN_EPS = 1e-5
LAG_STATES = 1
LAG_INVERSE = 2
LAG_RATIO = 3
LAG_TURN_Y = 6
LAG_RESIDUAL = 7
LAG_NORM = 8
LAG_HIGH = 9
LAG_LOW = 10
LAG_LOGIT = 11
U_MAX = 78.0
C_MAX = 15.0
X_SCALE = 1024.0


def wait(eng, sem, value):
    if not (isinstance(value, int) and value <= 0):
        eng.wait_ge(sem, value)


def wkv_moe_kernel(nc, x, ctx_in, time_decay, time_first, gate_w, w1, b1, w2, b2, out):
    B, T, C = x.shape
    E, _, DFF = w1.shape
    TOPK = 2
    N = B * T
    TILES = N // P
    CT = C // P
    GB = 4
    GT = GB * P
    NG = TILES // GB
    RB = GT // T
    SEG = T + 1
    FC = 512
    FT = FC // P
    CPE = DFF // FC
    NCH = TOPK * CPE
    NB = N // GT
    HID, W2, NS = FT, FT + 1, FT + 2
    assert NB == 4 and FT == 4 and CT == 4 and GB == 4 and C == 512 and NCH % 2 == 0

    x_v = x.rearrange("b t c -> (b t) c").rearrange("(n p) c -> p n c", p=P)
    v_v = ctx_in.rearrange("b t c -> (b t) c").rearrange("(n p) c -> p n c", p=P)
    out_v = out.rearrange("b t c -> (b t) c").rearrange("(n p) c -> p n c", p=P)

    with ExitStack() as ctx:
        def sb(name, shape, dt):
            return ctx.enter_context(nc.sbuf_tensor(name, shape, dt))

        def sem(name):
            return ctx.enter_context(nc.semaphore(name))

        xa = sb("xa", [P, TILES, C], F32)
        xh = sb("xh", [P, CT, N], F16)
        xl = sb("xl", [P, CT, N], F16)
        stage1 = sb("stage1", [P, CT, FC], F32)
        stage2 = sb("stage2", [P, FT, C], F32)
        ident = sb("ident", [P, P], F32)
        ones = sb("ones", [P, P], F32)
        rows = sb("rows", [P, P], F32)
        b1rows = sb("b1rows", [P, P], F32)
        gate_rows = sb("gate_rows", [E, C], F32)
        cols = sb("cols", [P, 2 * CT], F32)
        edec = sb("edec", [P, CT], F32)
        dcol = sb("dcol", [P, CT], F32)
        bonus = sb("bonus", [P, CT], F32)
        half = sb("half", [P, CT], F32)
        shift = sb("shift", [P, CT], F32)
        minus_c = sb("minus_c", [P, CT], F32)
        u_minus_c = sb("u_minus_c", [P, CT], F32)
        ebonus = sb("ebonus", [P, CT], F32)
        mask = sb("mask", [P, RB * SEG], F32)
        decay = sb("decay", [P, CT, RB * SEG], F32)
        eps = sb("eps", [P, 1], F32)
        b1T = sb("b1T", [P, E, DFF // P], F32)
        gT = sb("gT", [P, CT, E], F32)
        gres = sb("gres", [P, 2, CT, E], F32)
        g3 = sb("g3", [P, CT, 3, E], BF16)
        bn = sb("bn", [P, GB, 6], F32)
        mv = sb("mv", [P, TILES, 2], F32)
        lnv = sb("lnv", [P, TILES], F32)
        rstd = sb("rstd", [P, TILES], F32)
        nmr = sb("nmr", [P, TILES], F32)
        sm = sb("sm", [P, TILES], F32)
        nm = sb("nm", [P, TILES], F32)
        ssq = sb("ssq", [P, TILES], F32)
        lnv2 = sb("lnv2", [P, TILES], F32)
        rs2 = sb("rs2", [P, TILES], F32)
        logits = sb("logits", [P, TILES, E], F32)
        tot = sb("tot", [P, E], F32)
        top = sb("top", [P, 8], F32)
        topi = sb("topi", [P, 8], U32)
        topf = sb("topf", [P, 8], F32)
        iota = sb("iota", [P, E], F32)
        pick = sb("pick", [P, TOPK, E], F32)
        lsel = sb("lsel", [P, TOPK, TILES], F32)
        lmax = sb("lmax", [P, TILES], F32)
        lexp = sb("lexp", [P, TOPK, TILES], F32)
        lsum = sb("lsum", [P, TILES], F32)
        linv = sb("linv", [P, TILES], F32)
        rw = sb("rw", [P, TOPK, TILES], F32)
        ptmp = sb("ptmp", [P, TOPK, TILES, E], F32)
        b1tmp = sb("b1tmp", [P, TOPK, DFF // P, E], F32)
        b1c = sb("b1c", [P, TOPK, DFF // P], F32)
        mb = sb("mb", [P, TOPK], F32)
        mb2 = sb("mb2", [P, NCH], F32)
        mx = sb("mx", [P, NCH, NS], F32)
        q = sb("q", [P, NCH, NS], F32)
        mq = sb("mq", [P, NCH], F32)
        eb = sb("eb", [P, 2, NS], I32)
        scale = sb("scale", [P, 2, NS], F32)
        descale = sb("descale", [P, 2, NS], F32)
        gsc = sb("gsc", [P, 2, FT], F32)
        bias = sb("bias", [P, 2, FT], F32)
        rwc = sb("rwc", [P, NCH, TILES], F32)
        rwd = sb("rwd", [P, 2, TILES], F32)

        TP = CT * RB * SEG
        TU = CT * GT
        arena_y = sb("arena_y", [P, NG * TU], F32)
        arena_v = sb("arena_v", [P, NG * TU], F32)
        arena_t = sb("arena_t", [P, TU + 3 * TP], F32)
        arena_s = sb("arena_s", [P, 3 * C], F32)
        kn = arena_y[:, :].rearrange("p (g t c) -> p g t c", g=NG, t=GB)
        yT = arena_y[:, :].rearrange("p (g k n) -> p g k n", g=NG, k=CT)
        vn = arena_v[:, :].rearrange("p (n c) -> p n c", c=C)
        ek = arena_t[:, 0:TU].rearrange("p (k n) -> p k n", k=CT)
        s1, eav, sv = [arena_t[:, TU + i * TP:TU + (i + 1) * TP].rearrange("p (k n) -> p k n", k=CT) for i in range(3)]
        x2n = arena_s[:, 0:2 * C].rearrange("p (a c) -> p a c", a=2)
        junk = arena_s[:, 2 * C:3 * C]
        yb = arena_y[:, :].bitcast(F16)
        WS = CT * FC
        w1h = yb[:, 0:2 * WS].rearrange("p (a k f) -> p a k f", a=2, k=CT)
        w1l = yb[:, 2 * WS:4 * WS].rearrange("p (a k f) -> p a k f", a=2, k=CT)
        w2h = yb[:, 4 * WS:6 * WS].rearrange("p (a k f) -> p a k f", a=2, k=FT)
        w2l = yb[:, 6 * WS:8 * WS].rearrange("p (a k f) -> p a k f", a=2, k=FT)
        vb = arena_v[:, :].bitcast(F16)
        HS = NB * FT * GT
        hh = vb[:, 0:HS].rearrange("p (n k t) -> p n k t", n=NB, k=FT)
        hl = vb[:, HS:2 * HS].rearrange("p (n k t) -> p n k t", n=NB, k=FT)
        g32 = arena_t[:, 0:FT * GT].rearrange("p (k t) -> p k t", k=FT)
        b2b = arena_t[:, TU:TU + TOPK * C].rearrange("p (k c) -> p k c", k=TOPK)
        bt = arena_t[:, TU + TOPK * C:TU + 2 * TOPK * C].rearrange("p (k c) -> p k c", k=TOPK)

        ps = ctx.enter_context(nc.psum_tensor("ps", [P, 8, 512], F32))
        psK = [ps[:, 0, :], ps[:, 1, :]]
        psV = [ps[:, 2, :], ps[:, 3, :]]
        psY = ps[:, 4, :]
        psX = [ps[:, 5, :], ps[:, 6, :]]
        psM = ps[:, 7, :]
        psA = [ps[:, n, :] for n in range(FT)]
        psB = [ps[:, 4, :], ps[:, 5, :], ps[:, 7, :], ps[:, 5, :]]
        psS = ps[:, 6, 0:NS]

        d_x0 = [sem(f"d_x0_{t}") for t in range(GB)]
        d_x = [sem(f"d_x{g}") for g in range(1, NG)]
        d_v = [sem(f"d_v{g}") for g in range(NG)]
        d_rows = sem("d_rows")
        d_gate = sem("d_gate")
        d_w1f = [sem(f"d_w1f{f}") for f in range(FT)]
        d_w1 = sem("d_w1")
        d_w2 = sem("d_w2")
        d_b2 = sem("d_b2")
        d_out = sem("d_out")
        c_pool = sem("c_pool")
        c_id = sem("c_id")
        c_cols = sem("c_cols")
        c_rowsT = sem("c_rowsT")
        c_edec = sem("c_edec")
        c_dcol = sem("c_dcol")
        c_dve = sem("c_dve")
        c_bonus = sem("c_bonus")
        c_gateT = sem("c_gateT")
        c_g3 = sem("c_g3")
        c_ready = sem("c_ready")
        bn_done = sem("bn_done")
        mv_ready = sem("mv_ready")
        lnv_done = sem("lnv_done")
        rstd_ready = sem("rstd_ready")
        nmr_ready = sem("nmr_ready")
        kn_ready = sem("kn_ready")
        kT_ready = sem("kT_ready")
        vT_ready = sem("vT_ready")
        k1_ready = sem("k1_ready")
        keys_ready = sem("keys_ready")
        v_used = sem("v_used")
        sv_ready = sem("sv_ready")
        s1_ready = sem("s1_ready")
        num_done = sem("num_done")
        den_done = sem("den_done")
        lnd_done = sem("lnd_done")
        r_ready = sem("r_ready")
        y_done = sem("y_done")
        yT_ready = sem("yT_ready")
        x1_ready = sem("x1_ready")
        nm_ready = sem("nm_ready")
        sq_done = sem("sq_done")
        lnv2_done = sem("lnv2_done")
        rs2_ready = sem("rs2_ready")
        x2n_ready = sem("x2n_ready")
        x2T_ready = sem("x2T_ready")
        xh_ready = sem("xh_ready")
        xl_ready = sem("xl_ready")
        lg_mm = sem("lg_mm")
        lg_done = sem("lg_done")
        tot_mm = sem("tot_mm")
        rt = sem("rt")
        top_ready = sem("top_ready")
        l_ready = sem("l_ready")
        lexp_ready = sem("lexp_ready")
        rw_ready = sem("rw_ready")
        rwd_ready = sem("rwd_ready")
        mx_done = sem("mx_done")
        q_ready = sem("q_ready")
        sum_ready = sem("sum_ready")
        eb_ready = sem("eb_ready")
        de_ready = sem("de_ready")
        gsc_ready = sem("gsc_ready")
        bias_ready = sem("bias_ready")
        sc_ready = sem("sc_ready")
        w1h_ready = sem("w1h_ready")
        w1l_ready = sem("w1l_ready")
        w2h_ready = sem("w2h_ready")
        w2l_ready = sem("w2l_ready")
        up_mm = sem("up_mm")
        g_ready = sem("g_ready")
        hh_ready = sem("hh_ready")
        hl_ready = sem("hl_ready")
        down_mm = sem("down_mm")
        b2_step = sem("b2_step")
        b2_done = sem("b2_done")
        acc_done = sem("acc_done")

        block = ctx.enter_context(nc.Block())

        assert LAG_TURN_Y >= LAG_RATIO + CT - 1
        STEPS = TILES + LAG_LOGIT

        def y_bank(t):
            return psY if t < TILES - GB else (psK + psV)[t % GB]

        def at(s, lag):
            return s - lag if 0 <= s - lag < TILES else None

        pe_engine = nc.tensor

        def nothing(*_):
            pass

        def walk_chunks(eng, up, down, early_w1, early_w2, prepare, start):
            def pair(c, last):
                for par in range(2):
                    more = not (last and par == 1)
                    if more:
                        early_w1(c + par + 1, 1 - par)
                    up(c + par, par, 1)
                    if more:
                        early_w2(c + par + 1, 1 - par)
                    down(c + par, par, 0)
                    if more:
                        prepare(c + par + 1, 1 - par)
                    if eng is pe_engine:
                        with eng.Fori(1, NB - 1) as n:
                            up(c + par, par, n + 1)
                            down(c + par, par, n)
                    else:
                        for n in range(1, NB - 1):
                            up(c + par, par, n + 1)
                            down(c + par, par, n)
                    if more:
                        up(c + par + 1, 1 - par, 0)
                    down(c + par, par, NB - 1)

            start()
            with eng.Fori(0, NCH // 2 - 1) as i:
                pair(2 * i, False)
            pair(NCH - 2, True)

        @block.sync
        def _(sp):
            for t in range(GB):
                sp.dma_start(xa[:, t, :], x_v[:, t, :]).then_inc(d_x0[t], 16)
            for g in range(NG):
                if g + 1 < NG:
                    sp.dma_start(xa[:, (g + 1) * GB:(g + 2) * GB, :],
                                 x_v[:, (g + 1) * GB:(g + 2) * GB, :]).then_inc(d_x[g], 16)
                sp.dma_start(vn[:, g * GB:(g + 1) * GB, :], v_v[:, g * GB:(g + 1) * GB, :]).then_inc(d_v[g], 16)

            sp.wait_ge(top_ready, 1)
            picked = [sp.value_load(topi[0:1, 0:1], min_val=0, max_val=E - 1)]

            def w1_part(k, j):
                return w1[bass.ds(picked[k], 1), :, bass.ds(j * FC, FC)].rearrange("e (k p) f -> p (e k) f", p=P)

            def w2_part(k, j):
                return w2[bass.ds(picked[k], 1), bass.ds(j * FC, FC), :].rearrange("e (k p) d -> p (e k) d", p=P)

            def load_chunk(k, j, c):
                sp.wait_ge(w1h_ready, c * FT)
                sp.wait_ge(w1l_ready, c * FT)
                sp.dma_start(stage1[:, :, :], w1_part(k, j)).then_inc(d_w1, 16)
                sp.wait_ge(w2h_ready, c)
                sp.wait_ge(w2l_ready, c)
                sp.dma_start(stage2[:, :, :], w2_part(k, j)).then_inc(d_w2, 16)

            for f in range(FT):
                sp.dma_start(stage1[:, :, f * P:(f + 1) * P],
                             w1[bass.ds(picked[0], 1), :, f * P:(f + 1) * P]
                             .rearrange("e (k p) f -> p (e k) f", p=P)).then_inc(d_w1f[f], 16)
            sp.dma_start(stage2[:, :, :], w2_part(0, 0)).then_inc(d_w2, 16)
            picked.append(sp.value_load(topi[0:1, 1:2], min_val=0, max_val=E - 1))
            for k in range(TOPK):
                sp.dma_start(b2b[:, k, :], b2[bass.ds(picked[k], 1), :].broadcast_to([P, C])).then_inc(d_b2, 16)
            with sp.Fori(1, CPE) as j:
                load_chunk(0, j, j)
            with sp.Fori(0, CPE) as j:
                load_chunk(1, j, j + CPE)
            with sp.Fori(0, TILES) as t:
                sp.wait_ge(acc_done, t + NCH * TILES + 1)
                sp.dma_start(out_v[:, bass.ds(t, 1), :], xa[:, bass.ds(t, 1), :]).then_inc(d_out, 16)
            sp.wait_ge(d_out, 16 * TILES)

        @block.gpsimd
        def _(pool):
            nc.gpsimd.memset(ident[:, :], 0.0).then_inc(c_pool, 1)
            pool.wait_ge(c_pool, 1)
            nc.gpsimd.affine_select(out=ident[:, :], in_=ident[:, :], compare_op=ALU.not_equal, fill=1.0,
                                    base=0, pattern=[[-1, P]], channel_multiplier=1).then_inc(c_id, 1)
            nc.gpsimd.memset(ones[:, :], 1.0).then_inc(c_pool, 1)
            nc.gpsimd.memset(eps[:, :], LN_EPS).then_inc(c_pool, 1)
            nc.gpsimd.memset(mask[:, :], 1.0).then_inc(c_pool, 1)
            pool.wait_ge(c_pool, 4)
            nc.gpsimd.memset(mask[:, :].rearrange("p (b n) -> p b n", n=SEG)[:, :, 0:2], 0.0).then_inc(c_pool, 1)
            nc.gpsimd.memset(s1.rearrange("p k (b n) -> p (k b) n", n=SEG)[:, :, 0:1], 1.0).then_inc(c_pool, 1)
            for e in range(E):
                nc.gpsimd.memset(iota[:, e:e + 1], float(e)).then_inc(c_pool, 1)

            def rows_of(buf, j):
                return buf[:, j, :].rearrange("p (b n) -> p b n", n=T)

            def padded(buf, j):
                return buf[:, j, :].rearrange("p (b n) -> p b n", n=SEG)

            def denominator(u):
                j = u % CT
                pool.wait_ge(keys_ready, u + 1)
                pool.wait_ge(s1_ready, u + 1)
                nc.gpsimd.tensor_tensor(rows_of(ek, j), rows_of(ek, j), padded(s1, j)[:, :, 0:T],
                                        ALU.add).then_inc(den_done, 1)

            def ratio(u):
                g, j = divmod(u, CT)
                pool.wait_ge(r_ready, u + 1)
                pool.wait_ge(num_done, u + 1)
                if j == 0:
                    pool.wait_ge(kT_ready, g * CT + CT)
                nc.gpsimd.tensor_tensor(rows_of(yT[:, g], j), padded(eav, j)[:, :, 1:SEG], rows_of(ek, j),
                                        ALU.mult).then_inc(y_done, 1)

            def second_norm(t):
                pool.wait_ge(rs2_ready, t + 1)
                wait(pool, x2T_ready, t - 1)
                nc.gpsimd.tensor_scalar(x2n[:, t % 2, :], xa[:, t, :], nm[:, t:t + 1], rs2[:, t:t + 1],
                                        ALU.add, ALU.mult).then_inc(x2n_ready, 1)

            def first_norm(t):
                g, j = divmod(t, GB)
                pool.wait_ge(nmr_ready, g + 1)
                nc.gpsimd.tensor_scalar(kn[:, g, j, :], xa[:, t, :], rstd[:, t:t + 1], nmr[:, t:t + 1],
                                        ALU.mult, ALU.add).then_inc(kn_ready, 1)

            for t in (1, 3):
                first_norm(t)
            pool.wait_ge(c_g3, 1)
            nc.gpsimd.tensor_copy(g3[:, :, 0, :], gT[:, :, :]).then_inc(c_g3, 1)
            pool.wait_ge(c_g3, 2)
            nc.gpsimd.tensor_tensor(gres[:, 0, :, :], gT[:, :, :], g3[:, :, 0, :], ALU.subtract).then_inc(c_g3, 1)
            pool.wait_ge(c_g3, 3)
            nc.gpsimd.tensor_copy(g3[:, :, 1, :], gres[:, 0, :, :]).then_inc(c_g3, 1)
            pool.wait_ge(c_g3, 4)
            nc.gpsimd.tensor_tensor(gres[:, 1, :, :], gres[:, 0, :, :], g3[:, :, 1, :], ALU.subtract).then_inc(c_g3, 1)
            pool.wait_ge(c_g3, 5)
            nc.gpsimd.tensor_copy(g3[:, :, 2, :], gres[:, 1, :, :]).then_inc(c_g3, 1)

            for s in range(STEPS):
                if at(s, LAG_RATIO) is not None:
                    ratio(at(s, LAG_RATIO))
                if at(s, LAG_NORM) is not None:
                    second_norm(at(s, LAG_NORM))
                g, j = s // GB + 1, s % GB
                if g < NG and j < 3:
                    first_norm(g * GB + j)
                if at(s, LAG_STATES) is not None:
                    denominator(at(s, LAG_STATES))

            pool.wait_ge(rw_ready, TOPK)
            pool.wait_ge(d_b2, 16 * TOPK)
            with pool.Fori(0, TILES) as t:
                for k in range(TOPK):
                    nc.gpsimd.tensor_tensor(bt[:, k, :], b2b[:, k, :], rw[:, k, bass.ds(t, 1)].broadcast_to([P, C]),
                                            ALU.mult).then_inc(b2_step, 1)
                pool.wait_ge(b2_step, t * 3 + 2)
                nc.gpsimd.tensor_tensor(bt[:, 0, :], bt[:, 0, :], bt[:, 1, :], ALU.add).then_inc(b2_step, 1)
                pool.wait_ge(b2_step, t * 3 + 3)
                xt = xa[:, bass.ds(t, 1), :].rearrange("p a c -> p (a c)")
                nc.gpsimd.tensor_tensor(xt, xt, bt[:, 0, :], ALU.add).then_inc(b2_done, 1)
                pool.wait_ge(b2_done, t + 1)

        @block.scalar
        def _(act):
            nc.scalar.preload_act_table_set("natural_log_exp_and_others")
            act.dma_start(rows[0:CT, :], time_decay.rearrange("(k p) -> k p", p=P)).then_inc(d_rows, 16)
            act.dma_start(rows[CT:2 * CT, :], time_first.rearrange("(k p) -> k p", p=P)).then_inc(d_rows, 16)
            act.dma_start(gate_rows[:, :], gate_w).then_inc(d_gate, 16)
            act.dma_start(b1rows[:, :], b1.rearrange("e (k p) -> (e k) p", p=P)).then_inc(d_gate, 16)
            act.wait_ge(c_pool, 6 + E)

            def first_rstd(g):
                act.wait_ge(mv_ready, g * GB + GB)
                nc.scalar.activation(lnv[:, g * GB:(g + 1) * GB], mv[:, g * GB:(g + 1) * GB, 1],
                                     ACT.Ln, bias=eps[:, 0:1]).then_inc(lnv_done, 1)
                act.wait_ge(lnv_done, g + 1)
                nc.scalar.activation(rstd[:, g * GB:(g + 1) * GB], lnv[:, g * GB:(g + 1) * GB],
                                     ACT.Exp, scale=-0.5).then_inc(rstd_ready, 1)

            def first_norm(t):
                g, j = divmod(t, GB)
                act.wait_ge(nmr_ready, g + 1)
                nc.scalar.activation(kn[:, g, j, :], xa[:, t, :], ACT.Identity,
                                     scale=rstd[:, t:t + 1], bias=nmr[:, t:t + 1]).then_inc(kn_ready, 1)

            def keys(u):
                j = u % CT
                act.wait_ge(kT_ready, u + 1)
                wait(act, y_done, u - CT + 1)
                nc.scalar.activation(s1[:, j, :].rearrange("p (b n) -> p b n", n=SEG)[:, :, 1:SEG],
                                     psK[j % 2].rearrange("p (b n) -> p b n", n=T), ACT.Exp,
                                     bias=minus_c[:, j:j + 1]).then_inc(k1_ready, 1)
                nc.scalar.activation(ek[:, j, :], psK[j % 2], ACT.Exp, bias=u_minus_c[:, j:j + 1]).then_inc(keys_ready, 1)

            def variance_and_inverse(t, u):
                if t is not None:
                    act.wait_ge(nm_ready, t + 1)
                    wait(act, sq_done, t)
                    nc.scalar.activation(junk, xa[:, t, :], ACT.Square,
                                         bias=nm[:, t:t + 1], accum_out=ssq[:, t:t + 1]).then_inc(sq_done, 1)
                if u is not None:
                    den = ek[:, u % CT, :]
                    act.wait_ge(den_done, u + 1)
                    nc.scalar.activation(den, den, ACT.Ln).then_inc(lnd_done, 1)
                if t is not None:
                    act.wait_ge(sq_done, t + 1)
                    nc.scalar.activation(lnv2[:, t:t + 1], ssq[:, t:t + 1], ACT.Ln,
                                         bias=eps[:, 0:1], scale=1.0 / C).then_inc(lnv2_done, 1)
                if u is not None:
                    act.wait_ge(lnd_done, u + 1)
                    nc.scalar.activation(den, den, ACT.Exp, scale=-1.0).then_inc(r_ready, 1)
                if t is not None:
                    act.wait_ge(lnv2_done, t + 1)
                    nc.scalar.activation(rs2[:, t:t + 1], lnv2[:, t:t + 1], ACT.Exp,
                                         scale=-0.5).then_inc(rs2_ready, 1)

            def high(t):
                act.wait_ge(x2T_ready, t + 1)
                nc.scalar.activation(xh[:, :, t * P:(t + 1) * P], psX[t % 2].rearrange("p (k n) -> p k n", k=CT),
                                     ACT.Copy, scale=X_SCALE).then_inc(xh_ready, 1)

            first_rstd(0)
            act.wait_ge(c_cols, 1)
            nc.scalar.activation(edec[:, :], cols[:, 0:CT], ACT.Exp).then_inc(c_edec, 1)
            first_norm(0)
            act.wait_ge(c_edec, 1)
            nc.scalar.activation(dcol[:, :], edec[:, :], ACT.Exp, scale=-1.0).then_inc(c_dcol, 1)
            first_norm(2)
            act.wait_ge(c_bonus, 5)
            nc.scalar.activation(ebonus[:, :], bonus[:, :], ACT.Exp).then_inc(c_bonus, 1)
            first_rstd(1)
            for s in range(STEPS):
                if at(s, LAG_HIGH) is not None:
                    high(at(s, LAG_HIGH))
                if at(s, 0) is not None:
                    keys(at(s, 0))
                g, j = s // GB + 1, s % GB
                if g < NG and j == 2:
                    first_norm(g * GB + 3)
                if g + 1 < NG and j == 3:
                    first_rstd(g + 1)
                if at(s, LAG_INVERSE) == TILES - 1:
                    variance_and_inverse(None, TILES - 1)
                    variance_and_inverse(at(s, LAG_RESIDUAL), None)
                else:
                    variance_and_inverse(at(s, LAG_RESIDUAL), at(s, LAG_INVERSE))

            act.wait_ge(l_ready, TOPK)
            nc.scalar.activation(lexp[:, :, :], lsel[:, :, :], ACT.Exp, scale=1.0 / X_SCALE).then_inc(lexp_ready, 1)
            nc.scalar.preload_act_table(ACT.Gelu_apprx_tanh)

            def prepare(c, par):
                act.wait_ge(up_mm, (c - 1) * (NB * FT) + 1)
                act.wait_ge(sc_ready, c + NS)
                for f in range(FT):
                    high_w1(par, f)
                act.wait_ge(down_mm, c * TILES)
                high_w2(par)

            def high_w1(par, f):
                nc.scalar.activation(w1h[:, par, :, f * P:(f + 1) * P], stage1[:, :, f * P:(f + 1) * P],
                                     ACT.Identity, scale=scale[:, par, f:f + 1]).then_inc(w1h_ready, 1)

            def high_w2(par):
                nc.scalar.activation(w2h[:, par, :, :], stage2[:, :, :], ACT.Identity,
                                     scale=scale[:, par, W2:W2 + 1]).then_inc(w2h_ready, 1)

            def up(c, par, n):
                if isinstance(n, int) and n == 0:
                    act.wait_ge(gsc_ready, c + FT)
                    act.wait_ge(bias_ready, c + 1)
                for f in range(FT):
                    u = c * (NB * FT) + n * FT + f
                    act.wait_ge(up_mm, u + 1)
                    wait(act, hl_ready, u - FT + 1)
                    gelu(par, f)
                    act.wait_ge(g_ready, u + 1)
                    act.wait_ge(down_mm, c * TILES + n * GB + GB)
                    high_hidden(par, n, f)

            def gelu(par, f):
                nc.scalar.activation(g32[:, f, :], psA[f], ACT.Gelu_apprx_tanh, scale=gsc[:, par, f:f + 1],
                                     bias=bias[:, par, f:f + 1]).then_inc(g_ready, 1)

            def high_hidden(par, n, f):
                nc.scalar.activation(hh[:, n, f, :], g32[:, f, :], ACT.Identity,
                                     scale=scale[:, par, HID:HID + 1]).then_inc(hh_ready, 1)

            def start():
                for f in range(FT):
                    act.wait_ge(sc_ready, f + 1)
                    high_w1(0, f)
                act.wait_ge(bias_ready, 1)
                for f in range(FT):
                    act.wait_ge(gsc_ready, f + 1)
                    act.wait_ge(up_mm, f + 1)
                    gelu(0, f)
                    act.wait_ge(sc_ready, HID + 1)
                    act.wait_ge(g_ready, f + 1)
                    high_hidden(0, 0, f)
                act.wait_ge(sc_ready, W2 + 1)
                high_w2(0)

            walk_chunks(act, up, nothing, nothing, nothing, prepare, start)

        @block.vector
        def _(dve):
            def statistics(t):
                j = t % GB
                wait(dve, mv_ready, t - GB + 1)
                nc.vector.bn_stats(bn[:, j, :], xa[:, t, :]).then_inc(bn_done, 1)

            def aggregate(t):
                dve.wait_ge(bn_done, t + 1)
                nc.vector.bn_aggr(mv[:, t, :], bn[:, t % GB, :]).then_inc(mv_ready, 1)

            def minus_mean(g):
                dve.wait_ge(rstd_ready, g + 1)
                nc.vector.scalar_tensor_tensor(nmr[:, g * GB:(g + 1) * GB], mv[:, g * GB:(g + 1) * GB, 0], -1.0,
                                               rstd[:, g * GB:(g + 1) * GB], ALU.mult, ALU.mult).then_inc(nmr_ready, 1)

            def padded(buf, j):
                return buf[:, j, :].rearrange("p (b n) -> p b n", n=SEG)

            def starting_state(u):
                j = u % CT
                dve.wait_ge(vT_ready, u + 1)
                dve.wait_ge(k1_ready, u + 1)
                nc.vector.tensor_copy(padded(eav, j)[:, :, 0],
                                      psV[j % 2].rearrange("p (b n) -> p b n", n=T)[:, :, 0]).then_inc(v_used, 1)

            def terms(u):
                j = u % CT
                nc.vector.tensor_tensor(padded(eav, j)[:, :, 1:SEG], padded(s1, j)[:, :, 1:SEG],
                                        psV[j % 2].rearrange("p (b n) -> p b n", n=T), ALU.mult).then_inc(v_used, 1)

            def states(u):
                j = u % CT
                dve.wait_ge(v_used, 2 * u + 2)
                nc.vector.tensor_tensor_scan(sv[:, j, :], decay[:, j, :], eav[:, j, :], 0.0,
                                             ALU.mult, ALU.add).then_inc(sv_ready, 1)
                nc.vector.tensor_tensor_scan(s1[:, j, :], decay[:, j, :], s1[:, j, :], 0.0,
                                             ALU.mult, ALU.add).then_inc(s1_ready, 1)
                dve.wait_ge(sv_ready, u + 1)
                if u == 0:
                    dve.wait_ge(c_bonus, 6)
                nc.vector.scalar_tensor_tensor(padded(eav, j)[:, :, 1:SEG], padded(eav, j)[:, :, 1:SEG],
                                               ebonus[:, j:j + 1], padded(sv, j)[:, :, 0:T],
                                               ALU.mult, ALU.add).then_inc(num_done, 1)

            def residual(t):
                dve.wait_ge(yT_ready, t + 1)
                nc.vector.scalar_tensor_tensor(xa[:, t, :], y_bank(t), 1.0, xa[:, t, :], ALU.mult, ALU.add,
                                               accum_out=sm[:, t:t + 1]).then_inc(x1_ready, 1)

            def minus_second_mean(t):
                dve.wait_ge(x1_ready, t + 1)
                nc.vector.tensor_scalar(nm[:, t:t + 1], sm[:, t:t + 1], -1.0 / C, None, ALU.mult).then_inc(nm_ready, 1)

            def low(t):
                dve.wait_ge(xh_ready, t + 1)
                nc.vector.scalar_tensor_tensor(xl[:, :, t * P:(t + 1) * P],
                                               psX[t % 2].rearrange("p (k n) -> p k n", k=CT), X_SCALE,
                                               xh[:, :, t * P:(t + 1) * P], ALU.mult, ALU.subtract).then_inc(xl_ready, 1)

            def logit(t):
                dve.wait_ge(lg_mm, t + 1)
                nc.vector.tensor_reduce(logits[:, t, :], psM[:, 0:3 * E].rearrange("p (s e) -> p e s", s=3), AX_X,
                                        ALU.add).then_inc(lg_done, 1)

            for t in range(GB):
                dve.wait_ge(d_x0[t], 16)
                statistics(t)
            for t in range(GB):
                aggregate(t)
            dve.wait_ge(c_rowsT, 1)
            nc.vector.tensor_copy(cols[:, :], psM[:, 0:2 * CT]).then_inc(c_cols, 1)
            minus_mean(0)
            dve.wait_ge(c_cols, 1)
            nc.vector.tensor_scalar(bonus[:, :], cols[:, CT:2 * CT], U_MAX, -U_MAX, ALU.min, ALU.max).then_inc(c_bonus, 1)
            dve.wait_ge(c_bonus, 1)
            nc.vector.tensor_scalar(half[:, :], bonus[:, :], 0.5, -C_MAX, ALU.mult, ALU.max).then_inc(c_bonus, 1)
            dve.wait_ge(c_bonus, 2)
            nc.vector.scalar_tensor_tensor(shift[:, :], bonus[:, :], -C_MAX, half[:, :], ALU.add, ALU.max).then_inc(c_bonus, 1)
            dve.wait_ge(c_bonus, 3)
            nc.vector.tensor_scalar(minus_c[:, :], shift[:, :], -1.0, None, ALU.mult).then_inc(c_bonus, 1)
            nc.vector.tensor_tensor(u_minus_c[:, :], bonus[:, :], shift[:, :], ALU.subtract).then_inc(c_bonus, 1)
            dve.wait_ge(d_x[0], 16)
            for t in range(GB, 2 * GB):
                statistics(t)
            for t in range(GB, 2 * GB):
                aggregate(t)
            dve.wait_ge(c_pool, 6 + E)
            dve.wait_ge(c_dcol, 1)
            for j in range(CT):
                if j == 1:
                    minus_mean(1)
                nc.vector.tensor_scalar(decay[:, j, :], mask[:, :], dcol[:, j:j + 1], None, ALU.mult).then_inc(c_dve, 1)
            dve.wait_ge(c_gateT, 1)
            nc.vector.tensor_copy(gT[:, :, :], psM[:, 64:64 + CT * E].rearrange("p (k e) -> p k e", k=CT)).then_inc(c_g3, 1)
            nc.vector.tensor_copy(b1T[:, :, :].rearrange("p e f -> p (e f)"), psM[:, 128:256]).then_inc(c_ready, 1)
            dve.wait_ge(c_dve, CT)

            for s in range(STEPS):
                if s >= GB and s % GB == 0 and s // GB + 1 < NG:
                    minus_mean(s // GB + 1)
                n = s + 2 * GB
                if n < TILES:
                    dve.wait_ge(d_x[n // GB - 1], 16)
                    statistics(n)
                t, u = at(s, LAG_RESIDUAL), at(s, LAG_STATES)
                if t is not None:
                    residual(t)
                if u is not None:
                    starting_state(u)
                if t is not None:
                    minus_second_mean(t)
                if u is not None:
                    terms(u)
                if n < TILES:
                    aggregate(n)
                if at(s, LAG_LOW) is not None:
                    low(at(s, LAG_LOW))
                if u is not None:
                    states(u)
                if at(s, LAG_LOGIT) is not None:
                    logit(at(s, LAG_LOGIT))

            step = [0]

            def link(ins):
                step[0] += 1
                ins.then_inc(rt, 1)
                dve.wait_ge(rt, step[0])

            dve.wait_ge(tot_mm, 1)
            link(nc.vector.tensor_reduce(tot[:, :], psM[:, 128:128 + TILES * E].rearrange("p (t e) -> p e t", e=E),
                                         AX_X, ALU.add))
            link(nc.vector.max(top[:, :], tot[:, :]))
            nc.vector.max_index(topi[:, :], top[:, :], tot[:, :]).then_inc(top_ready, 1)
            dve.wait_ge(top_ready, 1)
            link(nc.vector.tensor_copy(topf[:, :], topi[:, :]))
            for k in range(TOPK):
                nc.vector.tensor_scalar(pick[:, k, :], iota[:, :], topf[:, k:k + 1], None, ALU.is_equal).then_inc(rt, 1)
            step[0] += TOPK
            dve.wait_ge(rt, step[0])
            for k in range(TOPK):
                nc.vector.tensor_tensor(ptmp[:, k, :, :], logits[:, :, :],
                                        pick[:, k:k + 1, :].broadcast_to([P, TILES, E]), ALU.mult).then_inc(rt, 1)
            step[0] += TOPK
            dve.wait_ge(rt, step[0])
            link(nc.vector.tensor_reduce(lsel[:, :, :], ptmp[:, :, :, :], AX_X, ALU.add))
            link(nc.vector.tensor_tensor(lmax[:, :], lsel[:, 0, :], lsel[:, 1, :], ALU.max))
            for k in range(TOPK):
                nc.vector.tensor_tensor(lsel[:, k, :], lsel[:, k, :], lmax[:, :], ALU.subtract).then_inc(l_ready, 1)
            for k in range(TOPK):
                nc.vector.tensor_tensor(b1tmp[:, k, :, :], b1T[:, :, :].rearrange("p e f -> p f e"),
                                        pick[:, k:k + 1, :].broadcast_to([P, DFF // P, E]), ALU.mult).then_inc(rt, 1)
            step[0] += TOPK
            dve.wait_ge(rt, step[0])
            link(nc.vector.tensor_reduce(b1c[:, :, :], b1tmp[:, :, :, :], AX_X, ALU.add))

            def bound_b1():
                link(nc.vector.tensor_reduce(mb[:, :], b1c[:, :, :], AX_X, ALU.max, apply_absolute_value=True))
                link(nc.vector.scalar_tensor_tensor(mb[:, :], mb[:, :], 4.0, mb[:, :], ALU.mult, ALU.mult))
                link(nc.vector.tensor_copy(mb2[:, :].rearrange("p (k c) -> p k c", k=TOPK),
                                           mb[:, :].rearrange("p (k c) -> p k c", c=1).broadcast_to([P, TOPK, CPE])))

            def router_weights():
                dve.wait_ge(lexp_ready, 1)
                link(nc.vector.tensor_tensor(lsum[:, :], lexp[:, 0, :], lexp[:, 1, :], ALU.add))
                link(nc.vector.reciprocal(linv[:, :], lsum[:, :]))
                for k in range(TOPK):
                    nc.vector.tensor_tensor(rw[:, k, :], lexp[:, k, :], linv[:, :], ALU.mult).then_inc(rw_ready, 1)
                dve.wait_ge(rw_ready, TOPK)
                for k in range(TOPK):
                    nc.vector.tensor_copy(rwc[:, k * CPE:(k + 1) * CPE, :],
                                          rw[:, k:k + 1, :].broadcast_to([P, CPE, TILES])).then_inc(rt, 1)
                step[0] += TOPK
                dve.wait_ge(rt, step[0])

            def scales(lo, hi, par, summed):
                dve.wait_ge(sum_ready, summed)
                nc.vector.tensor_scalar(eb[:, par, lo:hi], psS[:, lo:hi].bitcast(I32), 1, 0x7F800000,
                                        ALU.logical_shift_right, ALU.bitwise_and).then_inc(eb_ready, 1)
                dve.wait_ge(eb_ready, summed)
                nc.vector.tensor_scalar(scale[:, par, lo:hi].bitcast(I32), eb[:, par, lo:hi], -1.0,
                                        float((268 - 64) << 23), ALU.mult, ALU.add).then_inc(sc_ready, 1)
                return nc.vector.tensor_scalar(descale[:, par, lo:hi].bitcast(I32), eb[:, par, lo:hi],
                                               float((64 - 14) << 23), None, ALU.add)

            def undo_up(lo, hi, par):
                return nc.vector.tensor_scalar(gsc[:, par, lo:hi], descale[:, par, lo:hi], 1.0 / X_SCALE, None, ALU.mult)

            def low_w1(c, par, f):
                dve.wait_ge(w1h_ready, c * FT + f + 1)
                nc.vector.scalar_tensor_tensor(w1l[:, par, :, f * P:(f + 1) * P], stage1[:, :, f * P:(f + 1) * P],
                                               scale[:, par, f:f + 1], w1h[:, par, :, f * P:(f + 1) * P],
                                               ALU.mult, ALU.subtract).then_inc(w1l_ready, 1)

            def low_w2(c, par):
                dve.wait_ge(w2h_ready, c + 1)
                nc.vector.scalar_tensor_tensor(w2l[:, par, :, :], stage2[:, :, :], scale[:, par, W2:W2 + 1],
                                               w2h[:, par, :, :], ALU.mult, ALU.subtract).then_inc(w2l_ready, 1)

            def copy_bias(c, par):
                nc.vector.tensor_copy(bias[:, par, :], b1c[:, :, :].rearrange("p k f -> p (k f)")
                                      [:, bass.ds(c * FT, FT)]).then_inc(bias_ready, 1)

            def bound_tile(f):
                dve.wait_ge(d_w1f[f], 16)
                nc.vector.tensor_reduce(mx[:, 0, f:f + 1], stage1[:, :, f * P:(f + 1) * P], AX_XY, ALU.max,
                                        apply_absolute_value=True).then_inc(mx_done, 1)
                dve.wait_ge(mx_done, f + 1)
                nc.vector.scalar_tensor_tensor(q[:, 0, f:f + 1], mx[:, 0, f:f + 1], 2.0, mx[:, 0, f:f + 1],
                                               ALU.mult, ALU.mult).then_inc(q_ready, 1)

            def scale_tile(f):
                scales(f, f + 1, 0, f + 1).then_inc(de_ready, 1)
                dve.wait_ge(de_ready, f + 1)
                undo_up(f, f + 1, 0).then_inc(gsc_ready, 1)

            def start():
                copy_bias(0, 0)
                bound_tile(0)
                scale_tile(0)
                for f in range(1, FT):
                    bound_tile(f)
                    low_w1(0, 0, f - 1)
                    if f == FT - 1:
                        bound_b1()
                    scale_tile(f)
                low_w1(0, 0, FT - 1)
                dve.wait_ge(q_ready, FT)
                nc.vector.tensor_reduce(mq[:, 0:1], q[:, 0, 0:FT], AX_X, ALU.max).then_inc(mx_done, 1)
                dve.wait_ge(mx_done, FT + 1)
                nc.vector.scalar_tensor_tensor(q[:, 0, HID:HID + 1], mq[:, 0:1], 2.0 * C * CT, mb2[:, 0:1],
                                               ALU.mult, ALU.add).then_inc(q_ready, 1)
                scales(HID, HID + 1, 0, HID + 1).then_inc(de_ready, 1)
                dve.wait_ge(d_w2, 16)
                nc.vector.tensor_reduce(mx[:, 0, W2:W2 + 1], stage2[:, :, :], AX_XY, ALU.max,
                                        apply_absolute_value=True).then_inc(mx_done, 1)
                dve.wait_ge(mx_done, FT + 2)
                nc.vector.scalar_tensor_tensor(q[:, 0, W2:W2 + 1], mx[:, 0, W2:W2 + 1], 2.0, mx[:, 0, W2:W2 + 1],
                                               ALU.mult, ALU.mult).then_inc(q_ready, 1)
                router_weights()
                up(0, 0, 0)
                scales(W2, NS, 0, NS).then_inc(de_ready, 1)
                dve.wait_ge(de_ready, NS)
                low_w2(0, 0)

            def early_w1(c, par):
                dve.wait_ge(d_w1, c * 16)
                count = FT + 2 + (c - 1) * 3
                count_q = NS + (c - 1) * 3
                nc.vector.tensor_reduce(columns(mx, c, 0, FT),
                                        stage1[:, :, :].rearrange("p k (f u) -> p f k u", f=FT), AX_XY, ALU.max,
                                        apply_absolute_value=True).then_inc(mx_done, 1)
                dve.wait_ge(mx_done, count + 1)
                nc.vector.scalar_tensor_tensor(columns(q, c, 0, FT), columns(mx, c, 0, FT), 2.0, columns(mx, c, 0, FT),
                                               ALU.mult, ALU.mult).then_inc(q_ready, 1)
                dve.wait_ge(q_ready, count_q + 1)
                nc.vector.tensor_reduce(mq[:, bass.ds(c, 1)], columns(q, c, 0, FT), AX_X, ALU.max).then_inc(mx_done, 1)
                dve.wait_ge(mx_done, count + 2)
                nc.vector.scalar_tensor_tensor(columns(q, c, HID, HID + 1), mq[:, bass.ds(c, 1)], 2.0 * C * CT,
                                               mb2[:, bass.ds(c, 1)], ALU.mult, ALU.add).then_inc(q_ready, 1)

            def columns(buf, c, lo, hi):
                return buf[:, bass.ds(c, 1), lo:hi].rearrange("p a c -> p (a c)")

            def early_w2(c, par):
                dve.wait_ge(d_w2, c * 16 + 16)
                nc.vector.tensor_reduce(columns(mx, c, W2, NS), stage2[:, :, :], AX_XY, ALU.max,
                                        apply_absolute_value=True).then_inc(mx_done, 1)
                dve.wait_ge(mx_done, FT + 2 + c * 3)
                nc.vector.scalar_tensor_tensor(columns(q, c, W2, NS), columns(mx, c, W2, NS), 2.0, columns(mx, c, W2, NS),
                                               ALU.mult, ALU.mult).then_inc(q_ready, 1)

            def prepare(c, par):
                dve.wait_ge(g_ready, (c - 1) * (NB * FT) + 1)
                dve.wait_ge(hl_ready, (c - 1) * (NB * FT) + 1)
                copy_bias(c, par)
                scales(0, NS, par, c + NS).then_inc(de_ready, 1)
                dve.wait_ge(de_ready, c + NS)
                undo_up(0, FT, par).then_inc(gsc_ready, 1)
                for f in range(FT):
                    low_w1(c, par, f)
                low_w2(c, par)

            def up(c, par, n):
                for f in range(FT):
                    dve.wait_ge(hh_ready, c * (NB * FT) + n * FT + f + 1)
                    nc.vector.scalar_tensor_tensor(hl[:, bass.ds(n, 1), f, :].rearrange("p a t -> p (a t)"),
                                                   g32[:, f, :], scale[:, par, HID:HID + 1],
                                                   hh[:, bass.ds(n, 1), f, :].rearrange("p a t -> p (a t)"),
                                                   ALU.mult, ALU.subtract).then_inc(hl_ready, 1)

            def down(c, par, n):
                if n == 0:
                    nc.vector.tensor_scalar(rwd[:, par, :], rwc[:, bass.ds(c, 1), :].rearrange("p a c -> p (a c)"),
                                            descale[:, par, HID:HID + 1], descale[:, par, W2:W2 + 1], ALU.mult, ALU.mult).then_inc(rwd_ready, 1)
                    dve.wait_ge(rwd_ready, c + 1)
                for t in range(GB):
                    tile = n * GB + t
                    dve.wait_ge(down_mm, (c + 1) * TILES + tile + 1)
                    dve.wait_ge(b2_done, tile + 1)
                    dve.wait_ge(acc_done, c * TILES + tile + 1)
                    xt = xa[:, bass.ds(tile, 1), :].rearrange("p a c -> p (a c)")
                    nc.vector.scalar_tensor_tensor(xt, psB[t],
                                                   rwd[:, par, tile:tile + 1],
                                                   xt, ALU.mult, ALU.add).then_inc(acc_done, 1)

            dve.sem_inc(acc_done, TILES)
            walk_chunks(dve, up, down, early_w1, early_w2, prepare, start)

        @block.tensor
        def _(pe):
            pe.wait_ge(c_id, 1)
            pe.wait_ge(d_rows, 32)
            nc.tensor.transpose(psM[:, 0:2 * CT], rows[0:2 * CT, :], ident[0:2 * CT, 0:2 * CT]).then_inc(c_rowsT, 1)

            def turn_constants():
                pe.wait_ge(d_gate, 32)
                pe.wait_ge(c_cols, 1)
                for k in range(CT):
                    nc.tensor.transpose(psM[:, 64 + k * E:64 + (k + 1) * E], gate_rows[:, k * P:(k + 1) * P],
                                        ident[0:E, 0:E])
                nc.tensor.transpose(psM[:, 128:256], b1rows[:, :], ident[:, :]).then_inc(c_gateT, 1)

            def turn_k(u):
                g, j = divmod(u, CT)
                if j == 0:
                    pe.wait_ge(kn_ready, g * GB + GB)
                wait(pe, keys_ready, u - 1)
                for t in range(GB):
                    last = nc.tensor.transpose(psK[j % 2][:, t * P:(t + 1) * P], kn[:, g, t, j * P:(j + 1) * P],
                                               ident[:, :])
                last.then_inc(kT_ready, 1)

            def turn_v(u):
                g, j = divmod(u, CT)
                if j == 0:
                    pe.wait_ge(d_v[g], 16)
                wait(pe, v_used, 2 * u - 2)
                for t in range(GB):
                    last = nc.tensor.transpose(psV[j % 2][:, t * P:(t + 1) * P], vn[:, g * GB + t, j * P:(j + 1) * P],
                                               ident[:, :])
                last.then_inc(vT_ready, 1)

            def turn_y(t):
                g, j = divmod(t, GB)
                if j == 0:
                    pe.wait_ge(y_done, g * CT + CT)
                if y_bank(t) is psY:
                    wait(pe, x1_ready, t)
                for k in range(CT):
                    last = nc.tensor.transpose(y_bank(t)[:, k * P:(k + 1) * P], yT[:, g, k, j * P:(j + 1) * P], ident[:, :])
                last.then_inc(yT_ready, 1)

            def turn_x(t):
                pe.wait_ge(x2n_ready, t + 1)
                wait(pe, xl_ready, t - 1)
                for k in range(CT):
                    last = nc.tensor.transpose(psX[t % 2][:, k * P:(k + 1) * P], x2n[:, t % 2, k * P:(k + 1) * P],
                                               ident[:, :])
                last.then_inc(x2T_ready, 1)

            def router(t):
                pe.wait_ge(xl_ready, t + 1)
                wait(pe, lg_done, t)
                for n, part in enumerate((xh, xl)):
                    for k in range(CT):
                        last = nc.tensor.matmul(psM[:, 0:3 * E], part[:, k, t * P:(t + 1) * P],
                                                g3[:, k, :, :].rearrange("p s e -> p (s e)"),
                                                start=(n == 0 and k == 0), stop=(n == 1 and k == CT - 1))
                last.then_inc(lg_mm, 1)

            turn_constants()
            turn_k(0)
            turn_v(0)
            for s in range(STEPS):
                y = at(s, LAG_TURN_Y)
                if y is not None and y >= TILES - GB:
                    turn_y(y)
                if at(s, 0):
                    turn_v(at(s, 0))
                if s == LAG_LOGIT:
                    pe.wait_ge(c_g3, 6)
                    pe.wait_ge(c_ready, 1)
                if at(s, LAG_LOGIT) is not None:
                    router(at(s, LAG_LOGIT))
                if at(s + 1, 0) is not None:
                    turn_k(at(s + 1, 0))
                if y is not None and y < TILES - GB:
                    turn_y(y)
                if at(s, LAG_NORM) is not None:
                    turn_x(at(s, LAG_NORM))

            pe.wait_ge(lg_done, TILES)
            nc.tensor.matmul(psM[:, 128:128 + TILES * E], ones[:, :], logits[:, :, :].rearrange("p t e -> p (t e)"),
                             start=True, stop=True).then_inc(tot_mm, 1)

            def prepare(c, par):
                pe.wait_ge(q_ready, NS + c * 3)
                nc.tensor.matmul(psS, ones[:, :], q[:, bass.ds(c, 1), :].rearrange("p a c -> p (a c)"),
                                 start=True, stop=True).then_inc(sum_ready, 1)

            def keep_clock(count):
                for _ in range(count):
                    nc.tensor.matmul(psA[FT - 1], xh[:, 0, 0:P], xh[:, 0, 0:GT], start=True, stop=True)

            def sum_one(col):
                pe.wait_ge(q_ready, col + 1)
                nc.tensor.matmul(psS[:, col:col + 1], ones[:, :], q[:, 0, col:col + 1],
                                 start=True, stop=True).then_inc(sum_ready, 1)

            def up_tile(par, n, f):
                def tokens(part, k):
                    return part[:, k, bass.ds(n * GT, GT)]
                for k in range(CT):
                    a_h = w1h[:, par, k, f * P:(f + 1) * P]
                    a_l = w1l[:, par, k, f * P:(f + 1) * P]
                    nc.tensor.matmul(psA[f], a_h, tokens(xh, k), start=(k == 0), stop=False)
                    nc.tensor.matmul(psA[f], a_h, tokens(xl, k), start=False, stop=False)
                    last = nc.tensor.matmul(psA[f], a_l, tokens(xh, k), start=False, stop=(k == CT - 1))
                last.then_inc(up_mm, 1)

            def up(c, par, n):
                if isinstance(n, int) and n == 0:
                    pe.wait_ge(w1l_ready, c * FT + FT)
                for f in range(FT):
                    wait(pe, g_ready, c * (NB * FT) + n * FT + f - FT + 1)
                    up_tile(par, n, f)

            def start():
                sum_one(0)
                keep_clock(7)
                sum_one(1)
                for f in range(FT):
                    pe.wait_ge(w1h_ready, f + 1)
                    for k in range(CT):
                        a_h = w1h[:, 0, k, f * P:(f + 1) * P]
                        nc.tensor.matmul(psA[f], a_h, xh[:, k, 0:GT], start=(k == 0), stop=False)
                        nc.tensor.matmul(psA[f], a_h, xl[:, k, 0:GT], start=False, stop=False)
                    if f + 2 <= HID:
                        sum_one(f + 2)
                    pe.wait_ge(w1l_ready, f + 1)
                    for k in range(CT):
                        last = nc.tensor.matmul(psA[f], w1l[:, 0, k, f * P:(f + 1) * P], xh[:, k, 0:GT],
                                                start=False, stop=(k == CT - 1))
                    last.then_inc(up_mm, 1)
                sum_one(W2)

            def down(c, par, n):
                if isinstance(n, int) and n == 0:
                    pe.wait_ge(w2l_ready, c + 1)
                pe.wait_ge(hl_ready, c * (NB * FT) + n * FT + FT)
                for t in range(GB):
                    since = 2 if t % 2 else GB
                    pe.wait_ge(acc_done, (c + 1) * TILES + n * GB + t - since + 1)
                    for f in range(FT):
                        hid_h = hh[:, bass.ds(n, 1), f, t * P:(t + 1) * P].rearrange("p a t -> p (a t)")
                        hid_l = hl[:, bass.ds(n, 1), f, t * P:(t + 1) * P].rearrange("p a t -> p (a t)")
                        nc.tensor.matmul(psB[t], hid_h, w2h[:, par, f, :], start=(f == 0), stop=False)
                        nc.tensor.matmul(psB[t], hid_h, w2l[:, par, f, :], start=False, stop=False)
                        last = nc.tensor.matmul(psB[t], hid_l, w2h[:, par, f, :], start=False, stop=(f == FT - 1))
                    last.then_inc(down_mm, 1)

            keep_clock(16)
            pe.sem_inc(down_mm, TILES)
            walk_chunks(pe, up, down, nothing, nothing, prepare, start)


_INS = ['x', 'ctx_2048', 'L0_xattn_time_decay', 'L0_xattn_time_first', 'L0_ffn_gate_w', 'L0_ffn_w1', 'L0_ffn_b1',
        'L0_ffn_w2', 'L0_ffn_b2']
_OUTS = [((8, 256, 512), 'float32')]


def kernel(**inputs):
    import numpy as _np
    import concourse.bacc as _bacc
    from concourse import mybir as _mybir
    from concourse.bass_utils import run_bass_kernel_spmd as _run

    nc = _bacc.Bacc("TRN2", target_bir_lowering=False, num_devices=1)
    arrays, args = {}, []
    for name in _INS:
        a = _np.ascontiguousarray(inputs[name])
        arrays[f"in_{name}_dram"] = a
        args.append(nc.dram_tensor(f"in_{name}_dram", a.shape, _mybir.dt.from_np(a.dtype), kind="ExternalInput").ap())
    for i, (shape, dtype) in enumerate(_OUTS):
        dt = _mybir.dt.from_np(_np.dtype(dtype))
        args.append(nc.dram_tensor(f"out_{i}_dram", shape, dt, kind="ExternalOutput").ap())
    wkv_moe_kernel(nc, *args)
    r = _run(nc, [arrays], core_ids=[0])
    return r.results[0]["out_0_dram"]
```
